# Optimizing a Trainium2 kernel written in Bass

```python
import numpy as np
import jax
import jax.numpy as jnp

def _softmax(x, axis=-1):
    return jax.nn.softmax(x, axis=axis)

def _gelu(x):
    return jax.nn.gelu(x, approximate=True)

def _silu(x):
    return jax.nn.silu(x)

def _sigmoid(x):
    return jax.nn.sigmoid(x)

def _layernorm(x, axis=-1, eps=1e-05):
    m = jnp.mean(x, axis=axis, keepdims=True)
    v = jnp.var(x, axis=axis, keepdims=True)
    return (x - m) / jnp.sqrt(v + eps)

def _scatter_add(tgt, idx, src, axis=0):
    return tgt.at[idx].add(src)

def _segment_sum(src, seg, n):
    return jax.ops.segment_sum(src, seg, n)
kernel_name = 'mk_cond_resid_d2_seqx_r2_8f828c'

def setup_inputs(seed: int=0):
    np.random.seed(seed)
    _w = jnp.asarray

    def _rec_inputs():
        import jax
        import jax.numpy as jnp
        _rk = jax.random.key(seed)
        x = -0.0002919 + 1 * jax.random.normal(jax.random.fold_in(_rk, 1), (128, 128, 512), jnp.float32)
        _lenS = 128 - jax.random.randint(jax.random.fold_in(_rk, 7), (128,), 0, max(1, 128 // 4) + 1, jnp.int32)
        _lenS2 = 128 - jax.random.randint(jax.random.fold_in(_rk, 8), (128,), 0, max(1, 128 // 4) + 1, jnp.int32)
        cond_1024 = 0.0061147 + 1.02565 * jax.random.normal(jax.random.fold_in(_rk, 11), (128, 512), jnp.float32)
        _validS = jnp.arange(128)[None, :] < _lenS[:, None]
        _validS2 = jnp.arange(128)[None, :] < _lenS2[:, None]
        _causal = jnp.tril(jnp.ones((128, 128), dtype=bool))
        mask_Bx1x1xS_ff0 = jnp.where(jnp.ones((128, 1, 1, 128), dtype=bool), 0.0, -1000000000.0).astype(jnp.float32)
        return (x, cond_1024, mask_Bx1x1xS_ff0)
    x, cond_1024, mask_Bx1x1xS_ff0 = _rec_inputs()

    def _L0_cond_setup():
        import jax, jax.numpy as jnp
        import numpy as np
        EMBED = 512
        HEADS = 16
        HDIM = EMBED // HEADS
        MASK_OUT = -10000.0

        def _split_heads(t):
            B, T, _ = t.shape
            return t.reshape(B, T, HEADS, HDIM).transpose(0, 2, 1, 3)
        key = jax.random.key(seed)
        ks = jax.random.split(key, 12)
        B, S = (4, 1023)
        scale = 0.02
        return {'word_hidden_states': jax.random.normal(ks[0], (B, S, EMBED), jnp.float32), 'image_hidden_states': jax.random.normal(ks[1], (B, EMBED), jnp.float32), 'attention_mask': jnp.zeros((B, 1, 1, S), jnp.float32), 'c_attn_w': jax.random.normal(ks[2], (EMBED, 3 * EMBED), jnp.float32) * scale, 'c_attn_b': jnp.zeros((3 * EMBED,), jnp.float32), 'c_proj_w': jax.random.normal(ks[3], (EMBED, EMBED), jnp.float32) * scale, 'c_proj_b': jnp.zeros((EMBED,), jnp.float32), 'uk_w': jax.random.normal(ks[4], (EMBED, EMBED), jnp.float32) * scale, 'uk_b': jnp.zeros((EMBED,), jnp.float32), 'uv_w': jax.random.normal(ks[5], (EMBED, EMBED), jnp.float32) * scale, 'uv_b': jnp.zeros((EMBED,), jnp.float32)}
    _L0_cond_all = _L0_cond_setup()
    _L0_cond_in = {k: v for k, v in _L0_cond_all.items() if k in ('c_attn_w', 'c_attn_b', 'c_proj_w', 'c_proj_b', 'uk_w', 'uk_b', 'uv_w', 'uv_b')}
    del _L0_cond_all

    def _L1_cond_setup():
        import jax, jax.numpy as jnp
        import numpy as np
        import math
        IN_F = 512
        OUT_F = 512
        B = 16
        L = 2048
        key = jax.random.key(seed)
        k1, k2, k3 = jax.random.split(key, 3)
        Efou = jax.random.normal(k1, (B, L, IN_F), dtype=jnp.float32)
        y = jax.random.normal(k2, (B, IN_F), dtype=jnp.float32)
        weight = jax.random.normal(k3, (1, OUT_F, IN_F, 1), dtype=jnp.float32)
        return {'Efou': Efou, 'y': y, 'weight': weight}
    _L1_cond_all = _L1_cond_setup()
    _L1_cond_in = {k: v for k, v in _L1_cond_all.items() if k in ('weight',)}
    del _L1_cond_all
    return {'x': x, 'cond_1024': cond_1024, 'mask_Bx1x1xS_ff0': mask_Bx1x1xS_ff0, 'L0_cond_c_attn_w': _L0_cond_in['c_attn_w'], 'L0_cond_c_attn_b': _L0_cond_in['c_attn_b'], 'L0_cond_c_proj_w': _L0_cond_in['c_proj_w'], 'L0_cond_c_proj_b': _L0_cond_in['c_proj_b'], 'L0_cond_uk_w': _L0_cond_in['uk_w'], 'L0_cond_uk_b': _L0_cond_in['uk_b'], 'L0_cond_uv_w': _L0_cond_in['uv_w'], 'L0_cond_uv_b': _L0_cond_in['uv_b'], 'L1_cond_weight': _L1_cond_in['weight']}

def reference(x, cond_1024, mask_Bx1x1xS_ff0, L0_cond_c_attn_w, L0_cond_c_attn_b, L0_cond_c_proj_w, L0_cond_c_proj_b, L0_cond_uk_w, L0_cond_uk_b, L0_cond_uv_w, L0_cond_uv_b, L1_cond_weight):
    import jax
    import jax.numpy as jnp

    def _L0_cond_ref(word_hidden_states, image_hidden_states, attention_mask, c_attn_w, c_attn_b, c_proj_w, c_proj_b, uk_w, uk_b, uv_w, uv_b):
        import jax, jax.numpy as jnp
        import numpy as np
        EMBED = 512
        HEADS = 16
        HDIM = EMBED // HEADS
        MASK_OUT = -10000.0

        def _split_heads(t):
            B, T, _ = t.shape
            return t.reshape(B, T, HEADS, HDIM).transpose(0, 2, 1, 3)
        B, S, _ = word_hidden_states.shape
        qkv = word_hidden_states @ c_attn_w + c_attn_b
        q_word, k_word, v_word = jnp.split(qkv, 3, axis=-1)
        img = image_hidden_states[:, None, :]
        k_img = img @ uk_w.T + uk_b
        v_img = img @ uv_w.T + uv_b
        k = jnp.concatenate([k_img, k_word], axis=1)
        v = jnp.concatenate([v_img, v_word], axis=1)
        q = _split_heads(q_word)
        k = _split_heads(k)
        v = _split_heads(v)
        scores = jnp.einsum('bhqd,bhkd->bhqk', q, k) / jnp.sqrt(jnp.float32(HDIM))
        qi = jnp.arange(S)[:, None]
        kj = jnp.arange(S + 1)[None, :]
        causal = kj <= qi + 1
        scores = jnp.where(causal[None, None], scores, jnp.float32(MASK_OUT))
        zero_col = jnp.zeros(attention_mask.shape[:-1] + (1,), attention_mask.dtype)
        mask = jnp.concatenate([zero_col, attention_mask], axis=-1)
        scores = scores + mask
        attn = jax.nn.softmax(scores, axis=-1)
        out = jnp.einsum('bhqk,bhkd->bhqd', attn, v)
        out = out.transpose(0, 2, 1, 3).reshape(B, S, EMBED)
        out = out @ c_proj_w + c_proj_b
        return out

    def _L1_cond_ref(Efou, y, weight):
        import jax, jax.numpy as jnp
        import numpy as np
        import math
        IN_F = 512
        OUT_F = 512
        B = 16
        L = 2048
        b, img_size, in_f = Efou.shape
        out_f = weight.shape[1]
        scale = 1.0 / math.sqrt(in_f)
        w = scale * weight[:, :, :, 0] * y[:, None, :]
        dnorm = jax.lax.rsqrt(jnp.sum(w * w, axis=2, keepdims=True) + 1e-08)
        w = w * dnorm
        E = Efou.reshape(b, in_f, img_size)
        x = jnp.einsum('boi,bil->bol', w, E)
        return x.reshape(b, img_size, out_f)
    x = x + _L0_cond_ref(x, cond_1024, mask_Bx1x1xS_ff0, L0_cond_c_attn_w, L0_cond_c_attn_b, L0_cond_c_proj_w, L0_cond_c_proj_b, L0_cond_uk_w, L0_cond_uk_b, L0_cond_uv_w, L0_cond_uv_b)
    x = x + _L1_cond_ref(x, cond_1024, L1_cond_weight)
    return x

_drawn_inputs = setup_inputs


def setup_inputs(seed=0):
    import zlib

    import numpy as np

    out = dict(_drawn_inputs(seed))
    spreads = {'L0_cond_c_attn_b': (0.0, 0.1),
     'L0_cond_c_proj_b': (0.0, 0.1),
     'L0_cond_uk_b': (0.0, 2.0),
     'L0_cond_uv_b': (0.0, 0.8)}
    factors = {'L0_cond_uk_w': 8.0, 'L0_cond_uv_w': 3.849}
    for name, (base, spread) in spreads.items():
        noise = np.random.default_rng([zlib.crc32(name.encode()), seed]).standard_normal(out[name].shape)
        drawn = base * np.exp(spread * noise) if base else spread * noise
        out[name] = jnp.asarray(drawn.astype(out[name].dtype))
    for name, factor in factors.items():
        out[name] = (out[name] * factor).astype(out[name].dtype)
    return out
```

```python
from contextlib import ExitStack

import concourse.bass as bass
from concourse import mybir

ALU = mybir.AluOpType
ACT = mybir.ActivationFunctionType
F32 = mybir.dt.float32
F32R = mybir.dt.float32r

P = 128
NB = 128
PAIRS = NB // 2
E = 512
NC = E // P
HD = 32
HC = P // HD
H = E // HD
KEYS = P + 1
IMG = P
HALF = 2 * KEYS
MASK_OUT = -10000.0
LOWEST = -3.4e38
QSCALE = float(HD) ** -0.5
WSCALE = float(E) ** -0.5
EPS = 1e-8


class Pair:

    def __init__(self, t, k):
        self.t, self.k = t, k

    def at(self, d):
        return Pair(self.t, self.k + d)

    @property
    def slot(self):
        return self.k % 2

    def count(self, per, n):
        return self.t * (2 * per) + (self.k * per + n)

    def dma(self, n=1):
        return self.t * 16 + (self.k // 2 + n) * 16

    def batch(self):
        return self.t * 4 + self.k * 2


def build(nc, x, cond, mask, wqkv, bqkv, wproj, bproj, uk_w, uk_b, uv_w, uv_b, l1w, out):
    x_v = x.rearrange("b s e -> s b e")
    out_v = out.rearrange("b s e -> s b e")
    vrow_dram = nc.dram_tensor("v_rows", [NB, E], F32, kind="Internal").ap()

    with ExitStack() as ctx:
        def sb(name, shape, dt=F32):
            return ctx.enter_context(nc.sbuf_tensor(name, shape, dt))

        def sem(name):
            return ctx.enter_context(nc.semaphore(name))

        w_hi = sb("w_hi", [P, NC, 3 * E], F32R)
        w_lo = sb("w_lo", [P, NC, 3 * E], F32R)
        wp_hi = sb("wp_hi", [P, NC, E], F32R)
        wp_lo = sb("wp_lo", [P, NC, E], F32R)
        l_hi = sb("l_hi", [P, NC, NC, P], F32R)
        l_lo = sb("l_lo", [P, NC, NC, P], F32R)
        ident0 = sb("ident0", [P, P])
        ident = sb("ident", [P, P])
        qbias = sb("qbias", [P, NC])
        kbias = sb("kbias", [P, NC])
        ukbias = sb("ukbias", [P, NC])
        uvbias = sb("uvbias", [P, NC])
        pbias = sb("pbias", [P, E])
        kimgT = sb("kimgT", [P, NB, NC])
        vimgT = sb("vimgT", [P, NB, NC])
        ysc = sb("ysc", [P, NB, NC])
        dnorm = sb("dnorm", [P, NB, NC])
        vrow = sb("vrow", [P, 2, E])
        xin = sb("xin", [P, 2, 2, E])
        xb = sb("xb", [P, 2, 2, E])
        xT_hi = sb("xT_hi", [P, NC, 2, P], F32R)
        xT_lo = sb("xT_lo", [P, NC, 2, P], F32R)
        qT = sb("qT", [P, NC, 2 * P])
        kbd = sb("kbd", [P, 2, NC, HC, KEYS])
        v = sb("v", [P, 2, 2, E])
        S = [sb(f"S{b}", [P, H, KEYS]) for b in range(2)]
        pT = sb("pT", [P, 4, HC, P])
        aT_hi = sb("aT_hi", [P, 2, NC, P], F32R)
        aT_lo = sb("aT_lo", [P, 2, NC, P], F32R)
        yx = sb("yx", [P, NC, 2, P])
        yx_hi = sb("yx_hi", [P, NC, 2, P], F32R)
        yx_lo = sb("yx_lo", [P, NC, 2, P], F32R)
        maskb = sb("maskb", [P, 2, 2, KEYS])
        nmax = sb("nmax", [P, 2, H])
        pmax = sb("pmax", [P, 2, H])
        zsum = sb("zsum", [P, 2, H])
        rz = sb("rz", [P, 2, H])

        att = ctx.enter_context(nc.psum_tensor("att", [P, 4, 512], F32))
        A = ctx.enter_context(nc.psum_tensor("A", [P, 2, 512], F32))
        B = ctx.enter_context(nc.psum_tensor("B", [P, 2, 512], F32))

        uk_nat = kbd[:].rearrange("p b c h k -> p (b c h k)")[:, 0:2048].rearrange("p (o i) -> p o i", o=NC)
        uv_nat = kbd[:].rearrange("p b c h k -> p (b c h k)")[:, 2048:4096].rearrange("p (o i) -> p o i", o=NC)
        l_nat = pT[:].rearrange("p a b c -> p (a b c)").rearrange("p (o i) -> p o i", o=NC)
        ukT = v[:].rearrange("p a b e -> p (a b e)").rearrange("p (i o) -> p i o", i=NC)
        uvT = xb[:].rearrange("p a b e -> p (a b e)").rearrange("p (i o) -> p i o", i=NC)
        cond_nat = qT[:].rearrange("p c t -> p (c t)")[:, 0:E]
        condT = qT[:].rearrange("p c t -> p (c t)")[:, E:2 * E].rearrange("p (c b) -> p c b", c=NC)
        stage = [s[:].rearrange("p h k -> p (h k)") for s in S]
        w_sq = uk_nat.rearrange("p c (d s) -> p c d s", d=NC)
        ysq = yx[:].rearrange("p c b t -> p (c b t)")[:, 0:512].rearrange("p (c b) -> p c b", c=NC)
        dn_u, dn_r, dn_t = (uv_nat[:, n, :].rearrange("p (d b) -> p d b", d=NC) for n in range(3))
        vb_bc, uvb_bc, vrow_st = xin[:, 0, 0, :], xin[:, 0, 1, :], vrow[:, 0, :]

        w_loaded = [sem(f"w_loaded{n}") for n in range(2)]
        cond_loaded, uk_loaded, uv_loaded = sem("cond_loaded"), sem("uk_loaded"), sem("uv_loaded")
        l_loaded, bias_loaded = sem("l_loaded"), sem("bias_loaded")
        ident_ready = sem("ident_ready")
        w_hi_done, w_lo_done = sem("w_hi_done"), sem("w_lo_done")
        tr_done, tr_kept, l_lo_done = sem("tr_done"), sem("tr_kept"), sem("l_lo_done")
        qbias_scaled = sem("qbias_scaled")
        image_done, image_kept = sem("image_done"), sem("image_kept")
        vrow_ready, vrow_stored = sem("vrow_ready"), sem("vrow_stored")
        dn_sum, dn_step, dn_root = sem("dn_sum"), sem("dn_step"), sem("dn_root")
        kbd_zero = sem("kbd_zero")
        mask_zero = sem("mask_zero")

        x_loaded = [sem(f"x_loaded{n}") for n in range(2)]
        mask_loaded = [sem(f"mask_loaded{n}") for n in range(2)]
        stored = [sem(f"stored{n}") for n in range(2)]
        vrow_loaded = sem("vrow_loaded")
        xt_done = sem("xt_done")
        xhi_done = sem("xhi_done")
        xlo_done = sem("xlo_done")
        k_done, q_done, v_done = sem("k_done"), sem("q_done"), sem("v_done")
        k_kept, q_kept, v_kept = sem("k_kept"), sem("q_kept"), sem("v_kept")
        s_done, s_kept = sem("s_done"), sem("s_kept")
        sel_done = sem("sel_done")
        sel_seen, s_seen = sem("sel_seen"), sem("s_seen")
        rowmax_done, max_done = sem("rowmax_done"), sem("max_done")
        exp_done = sem("exp_done")
        rz_done = sem("rz_done")
        norm_done = sem("norm_done")
        pt_done, pt_kept = sem("pt_done"), sem("pt_kept")
        av_done = sem("av_done")
        ahi_done, alo_done = sem("ahi_done"), sem("alo_done")
        proj_done = sem("proj_done")
        xb_done = sem("xb_done")
        x1_done = sem("x1_done")
        yx_done = sem("yx_done")
        yhi_done, ylo_done = sem("yhi_done"), sem("ylo_done")
        l1_done = sem("l1_done")
        dn_done = sem("dn_done")
        out_done = sem("out_done")

        block = ctx.enter_context(nc.Block())

        def run_pairs(eng, step):
            step(Pair(0, 0), 0, 2)
            step(Pair(0, 1), 1, 2)
            with eng.Fori(0, PAIRS // 2 - 2) as t:
                for k in (2, 3):
                    step(Pair(t, k), 2, 2)
            step(Pair(0, PAIRS - 2), 2, 1)
            step(Pair(0, PAIRS - 1), 2, 0)

        LAST = Pair(0, PAIRS - 1)

        banks = [att[:, n] for n in range(4)] + [A[:, n] for n in range(2)] + [B[:, n] for n in range(2)]
        COND, Y, UK, UV, L1 = 0, 1, 2, 6, 10
        TR = 14

        @block.sync
        def _(sp):
            def load_x(p):
                sp.dma_start(xin[:, p.slot], x_v[:, bass.ds(p.batch(), 2), :]).then_inc(x_loaded[p.slot], 16)

            def load_mask(p):
                rows = mask[bass.ds(p.batch(), 2), 0, 0, :].partition_broadcast(P)
                sp.dma_start(maskb[:, p.slot, :, 0:P], rows).then_inc(mask_loaded[p.slot], 16)

            def load_vrow(p):
                rows = vrow_dram[bass.ds(p.batch(), 2), :].partition_broadcast(P)
                sp.dma_start(vrow[:], rows).then_inc(vrow_loaded, 16)

            wq_v = wqkv.rearrange("(c p) n -> p c n", p=P)
            sp.dma_start(cond_nat, cond).then_inc(cond_loaded, 16)
            sp.dma_start(uk_nat, uk_w.rearrange("(o p) i -> p o i", p=P)).then_inc(uk_loaded, 16)
            sp.dma_start(uv_nat, uv_w.rearrange("(o p) i -> p o i", p=P)).then_inc(uv_loaded, 16)
            sp.dma_start(l_nat, l1w[0, :, :, 0].rearrange("(s d) i -> s d i", d=NC)).then_inc(l_loaded, 16)
            for c in range(NC):
                if c >= 2:
                    sp.wait_ge(w_hi_done, c - 1)
                    sp.wait_ge(w_lo_done, c - 1)
                sp.dma_start(stage[c % 2][:, 0:3 * E], wq_v[:, c, :]).then_inc(w_loaded[c % 2], 16)
                if c == 1:
                    for dst, src in ((qbias, bqkv[0:E]), (kbias, bqkv[E:2 * E]), (ukbias, uk_b), (uvbias, uv_b)):
                        sp.dma_start(dst[:], src.rearrange("(c p) -> p c", p=P),
                                     allow_slow_non_contiguous=True).then_inc(bias_loaded, 16)
                    for dst, src in ((pbias[:], bproj), (vb_bc, bqkv[2 * E:3 * E]), (uvb_bc, uv_b)):
                        sp.dma_start(dst, src.partition_broadcast(P)).then_inc(bias_loaded, 16)
            sp.wait_ge(w_hi_done, NC - 1)
            sp.wait_ge(w_lo_done, NC - 1)
            sp.dma_start(stage[0][:, 0:NC * E].rearrange("p (c n) -> p c n", c=NC),
                         wproj.rearrange("(c p) n -> p c n", p=P)).then_inc(w_loaded[0], 16)
            sp.wait_ge(vrow_ready, 2)
            sp.dma_start(vrow_dram, vrow_st).then_inc(vrow_stored, 16)
            sp.wait_ge(mask_zero, 1)
            load_mask(Pair(0, 0))
            load_x(Pair(0, 0))
            load_x(Pair(0, 1))
            sp.wait_ge(vrow_stored, 16)
            load_vrow(Pair(0, 0))

            def store(q):
                sp.wait_ge(out_done, q.count(1, 1))
                sp.dma_start(out_v[:, bass.ds(q.batch(), 2), :], xb[:, q.slot]).then_inc(stored[q.slot], 16)

            def step(p, back, ahead):
                if ahead:
                    if back:
                        sp.wait_ge(max_done, p.at(-1).count(2, 2))
                    load_mask(p.at(1))
                    sp.wait_ge(v_kept, p.count(2, 2))
                    load_vrow(p.at(1))
                if ahead > 1:
                    sp.wait_ge(xb_done, p.count(1, 1))
                    load_x(p.at(2))
                if back:
                    store(p.at(-1))

            run_pairs(sp, step)
            store(LAST)
            for n in range(2):
                sp.wait_ge(stored[n], 16 * (PAIRS // 2))

        @block.gpsimd
        def _(pool):
            nc.gpsimd.memset(ident0[:], 0.0).then_inc(ident_ready, 1)
            pool.wait_ge(ident_ready, 1)
            nc.gpsimd.affine_select(out=ident[:], in_=ident0[:], compare_op=ALU.not_equal, fill=1.0, base=0,
                                    pattern=[[-1, P]], channel_multiplier=1).then_inc(ident_ready, 1)
            nc.gpsimd.memset(maskb[:, :, :, IMG:KEYS], 0.0).then_inc(mask_zero, 1)
            pool.wait_ge(dn_step, 6)
            nc.gpsimd.memset(kbd[:], 0.0).then_inc(kbd_zero, 1)

            mask_out = pool.to_reg(MASK_OUT)

            def scale_y(q):
                pool.wait_ge(x1_done, q.count(2, 2))
                nc.gpsimd.tensor_tensor(
                    yx[:].rearrange("p c b l -> p b c l"),
                    xb[:, q.slot].rearrange("p b (c l) -> p b c l", c=NC),
                    ysc[:, bass.ds(q.batch(), 2), :].unsqueeze(3).to_broadcast([P, 2, NC, P]),
                    ALU.mult).then_inc(yx_done, 1)

            def normalize(p, b):
                pool.wait_ge(rz_done, p.count(2, b + 1))
                for c in range(NC):
                    heads = slice(HC * c, HC * c + HC)
                    s = S[b][:, heads, 0:P]
                    nc.gpsimd.tensor_tensor(s, s, rz[:, b, heads].unsqueeze(2).to_broadcast([P, HC, P]),
                                            ALU.mult).then_inc(norm_done, 1)

            def add_bias(p, back):
                pool.wait_ge(x_loaded[p.slot], p.dma())
                if back == 0:
                    pool.wait_ge(bias_loaded, 16 * 7)
                    pool.wait_ge(image_done, 3)
                if back == 2:
                    pool.wait_ge(stored[p.slot], p.at(-2).dma())
                nc.gpsimd.tensor_tensor(xb[:, p.slot], xin[:, p.slot],
                                        pbias[:].unsqueeze(1).to_broadcast([P, 2, E]), ALU.add).then_inc(xb_done, 1)

            def add_out(q):
                pool.wait_ge(dn_done, q.count(1, 1))
                o = xb[:, q.slot].rearrange("p b (c l) -> p b c l", c=NC)
                nc.gpsimd.tensor_tensor(o, o, yx[:].rearrange("p c b l -> p b c l"), ALU.add).then_inc(out_done, 1)

            def step(p, back, ahead):
                for b in range(2):
                    for g in range(2):
                        pool.wait_ge(s_kept, p.count(8, 4 * b + 2 * g + 2))
                        pool.sem_inc(s_seen, 1)
                        s = S[b][:, 8 * g:8 * g + 8, 0:P]
                        nc.gpsimd.affine_select(out=s, in_=s, compare_op=ALU.is_ge, fill=mask_out, base=0,
                                                pattern=[[0, 8], [-1, P]], channel_multiplier=1)\
                            .then_inc(sel_done, 1)
                if back:
                    scale_y(p.at(-1))
                normalize(p, 0)
                add_bias(p, back)
                normalize(p, 1)
                if back:
                    add_out(p.at(-1))

            run_pairs(pool, step)
            pool.wait_ge(out_done, LAST.at(-1).count(1, 1))
            scale_y(LAST)
            add_out(LAST)

        @block.scalar
        def _(act):
            def kept(u, out_ap, in_ap, inc=True):
                act.wait_ge(tr_done, u + 1)
                i = nc.scalar.activation(out_ap, in_ap, ACT.Copy)
                return i.then_inc(tr_kept, 1) if inc else i

            def chunked(u):
                return banks[u % 8].rearrange("p (c n) -> p c n", c=NC)

            kept(COND, condT, chunked(COND))
            kept(Y, ysc[:].rearrange("p b c -> p c b"), chunked(Y), inc=False)
            nc.scalar.activation(ysq, chunked(Y), ACT.Square).then_inc(tr_kept, 1)
            for n in range(NC):
                kept(UK + n, ukT[:, n, :], banks[(UK + n) % 8])
            for n in range(NC):
                kept(UV + n, uvT[:, n, :], banks[(UV + n) % 8])
            for c in range(NC):
                kept(L1 + c, l_hi[:, c].rearrange("p d s -> p (d s)"), banks[(L1 + c) % 8], inc=False)
                nc.scalar.activation(w_sq[:, c].rearrange("p d s -> p (d s)"), banks[(L1 + c) % 8],
                                     ACT.Square).then_inc(tr_kept, 1)
            act.wait_ge(bias_loaded, 16 * 7)
            for n, (dst, bias, bank) in enumerate(((kimgT, ukbias, 6), (vimgT, uvbias, 7))):
                act.wait_ge(image_done, n + 1)
                for c in range(NC):
                    last = nc.scalar.activation(dst[:, :, c], banks[bank][:, P * c:P * c + P], ACT.Identity,
                                                bias=bias[:, c:c + 1])
                last.then_inc(image_kept, 1)
            for c in range(NC):
                act.wait_ge(w_loaded[c % 2], 16 * (c // 2 + 1))
                nc.scalar.activation(w_hi[:, c, :], stage[c % 2][:, 0:3 * E], ACT.Copy).then_inc(w_hi_done, 1)
            act.wait_ge(w_loaded[0], 16 * 3)
            nc.scalar.activation(wp_hi[:].rearrange("p c n -> p (c n)"), stage[0][:, 0:NC * E],
                                 ACT.Copy).then_inc(w_hi_done, 1)
            act.wait_ge(dn_step, 1)
            nc.scalar.activation(dn_r, dn_u, ACT.Sqrt).then_inc(dn_root, 1)

            def keep_xT_hi(p):
                act.wait_ge(xt_done, p.count(2, 2))
                nc.scalar.activation(xT_hi[:].rearrange("p e b t -> p b e t"),
                                     A[:].rearrange("p b (e t) -> p b e t", e=NC), ACT.Copy).then_inc(xhi_done, 1)

            def keep_q(p):
                for c in range(NC):
                    if c % 2 == 0:
                        act.wait_ge(q_done, p.count(2, c // 2 + 1))
                    last = nc.scalar.activation(qT[:, c, :], B[:, c // 2, 256 * (c % 2):256 * (c % 2) + 256],
                                                ACT.Identity, bias=qbias[:, c:c + 1], scale=QSCALE)
                    if c % 2:
                        last.then_inc(q_kept, 1)

            def exps(p, b):
                act.wait_ge(max_done, p.count(2, b + 1))
                for h in range(H):
                    last = nc.scalar.activation(S[b][:, h, :], S[b][:, h, :], ACT.Exp, bias=nmax[:, b, h:h + 1],
                                                accum_out=zsum[:, b, h:h + 1])
                last.then_inc(exp_done, 1)

            def keep_yx_hi(q):
                act.wait_ge(yx_done, q.count(1, 1))
                nc.scalar.activation(yx_hi[:], yx[:], ACT.Copy).then_inc(yhi_done, 1)

            keep_xT_hi(Pair(0, 0))
            act.wait_ge(qbias_scaled, 1)
            keep_q(Pair(0, 0))

            def step(p, back, ahead):
                for n in range(8):
                    act.wait_ge(s_done, p.count(8, n + 1))
                    c = n % 4
                    nc.scalar.activation(S[n // 4][:, HC * c:HC * c + HC, :].rearrange("p (a h) k -> p a (h k)", a=2),
                                         att[:, 2 * (n % 2):2 * (n % 2) + 2, 0:HALF], ACT.Copy).then_inc(s_kept, 1)
                if ahead:
                    keep_xT_hi(p.at(1))
                exps(p, 0)
                if back:
                    keep_yx_hi(p.at(-1))
                exps(p, 1)
                if ahead:
                    keep_q(p.at(1))
                for n in range(8):
                    act.wait_ge(pt_done, p.count(8, n + 1))
                    if n >= 4 or back:
                        act.wait_ge(av_done, p.count(8, n - 3))
                    nc.scalar.activation(pT[:, n % 4].rearrange("p h q -> p (h q)"), att[:, n % 4, :],
                                         ACT.Copy).then_inc(pt_kept, 1)
                    if n == 6:
                        keep_aT_hi(p, 0)
                keep_aT_hi(p, 1)

            def keep_aT_hi(p, b):
                act.wait_ge(av_done, p.count(8, 4 * b + 4))
                for c in range(NC):
                    last = nc.scalar.activation(aT_hi[:, b, c, :], A[:, b, P * c:P * c + P], ACT.Identity,
                                                bias=vimgT[:, p.batch() + b, c:c + 1])
                last.then_inc(ahi_done, 1)

            run_pairs(act, step)
            keep_yx_hi(LAST)

        @block.vector
        def _(dve):
            def splits_low(out_ap, in_ap, hi_ap):
                return nc.vector.tensor_tensor(out_ap, in_ap, hi_ap.bitcast(F32), ALU.subtract)

            dve.wait_ge(bias_loaded, 16 * 7)
            nc.vector.tensor_scalar(qbias[:], qbias[:], QSCALE, None, ALU.mult).then_inc(qbias_scaled, 1)
            nc.vector.tensor_tensor(uvb_bc, vb_bc, uvb_bc, ALU.subtract).then_inc(vrow_ready, 1)
            for c in range(NC):
                dve.wait_ge(tr_kept, L1 + c + 1)
                splits_low(l_lo[:, c].rearrange("p d s -> p (d s)"), banks[(L1 + c) % 8],
                           l_hi[:, c].rearrange("p d s -> p (d s)")).then_inc(l_lo_done, 1)
            dve.wait_ge(image_done, 3)
            dve.wait_ge(vrow_ready, 1)
            nc.vector.tensor_tensor(vrow_st, uvb_bc, banks[0], ALU.subtract).then_inc(vrow_ready, 1)
            for c in range(NC):
                dve.wait_ge(w_loaded[c % 2], 16 * (c // 2 + 1))
                dve.wait_ge(w_hi_done, c + 1)
                splits_low(w_lo[:, c, :], stage[c % 2][:, 0:3 * E], w_hi[:, c, :]).then_inc(w_lo_done, 1)
            dve.wait_ge(w_loaded[0], 16 * 3)
            dve.wait_ge(w_hi_done, NC + 1)
            splits_low(wp_lo[:].rearrange("p c n -> p (c n)"), stage[0][:, 0:NC * E],
                       wp_hi[:].rearrange("p c n -> p (c n)")).then_inc(w_lo_done, 1)
            dve.wait_ge(dn_sum, 1)
            nc.vector.tensor_scalar(dn_u, banks[1].rearrange("p (d b) -> p d b", d=NC), WSCALE * WSCALE, EPS,
                                    ALU.mult, ALU.add).then_inc(dn_step, 1)
            dve.wait_ge(dn_root, 1)
            nc.vector.reciprocal(dn_t, dn_r).then_inc(dn_step, 1)
            dve.wait_ge(dn_step, 2)
            nc.vector.tensor_tensor(dn_r, dn_t, dn_t, ALU.mult).then_inc(dn_step, 1)
            dve.wait_ge(dn_step, 3)
            nc.vector.tensor_tensor(dn_r, dn_r, dn_u, ALU.mult).then_inc(dn_step, 1)
            dve.wait_ge(dn_step, 4)
            nc.vector.tensor_scalar(dn_r, dn_r, -0.5, 1.5, ALU.mult, ALU.add).then_inc(dn_step, 1)
            dve.wait_ge(dn_step, 5)
            nc.vector.scalar_tensor_tensor(out=dnorm[:].rearrange("p b d -> p d b"), in0=dn_t, scalar=WSCALE,
                                           in1=dn_r, op0=ALU.mult, op1=ALU.mult).then_inc(dn_step, 1)
            dve.wait_ge(dn_step, 6)

            def keep_xT_lo(p):
                dve.wait_ge(xhi_done, p.count(1, 1))
                splits_low(xT_lo[:].rearrange("p e b t -> p b e t"), A[:].rearrange("p b (e t) -> p b e t", e=NC),
                           xT_hi[:].rearrange("p e b t -> p b e t")).then_inc(xlo_done, 1)

            def keep_k(p):
                dve.wait_ge(k_done, p.count(1, 1))
                for j in range(HC):
                    q = slice(HD * j, HD * j + HD)
                    nc.vector.tensor_copy(kbd[q, :, :, j, IMG], kimgT[q, bass.ds(p.batch(), 2), :])
                    last = nc.vector.tensor_tensor(
                        kbd[q, :, :, j, 0:P].rearrange("p b c t -> p c b t"),
                        A[q].rearrange("p a (c b t) -> p (a c) b t", c=2, b=2),
                        kbias[q, :].unsqueeze(2).unsqueeze(3).to_broadcast([HD, NC, 2, P]), ALU.add)
                last.then_inc(k_kept, 1)

            def keep_v(p):
                dve.wait_ge(vrow_loaded, p.count(16, 16))
                for b in range(2):
                    dve.wait_ge(v_done, p.count(2, b + 1))
                    nc.vector.tensor_tensor(v[:, p.slot, b, :], B[:, b, :], vrow[:, b, :], ALU.add)\
                        .then_inc(v_kept, 1)

            def row_max(p, b):
                if b == 0:
                    dve.wait_ge(mask_loaded[p.slot], p.dma())
                for h in range(H):
                    if h % 8 == 0:
                        dve.wait_ge(sel_done, p.count(4, 2 * b + h // 8 + 1))
                        dve.sem_inc(sel_seen, 1)
                    last = nc.vector.tensor_tensor_reduce(
                        out=S[b][:, h, :], in0=S[b][:, h, :], in1=maskb[:, p.slot, b, :], scale=1.0, scalar=LOWEST,
                        op0=ALU.add, op1=ALU.max, accum_out=pmax[:, b, h:h + 1])
                last.then_inc(rowmax_done, 1)
                dve.wait_ge(rowmax_done, p.count(2, b + 1))
                nc.vector.tensor_scalar(nmax[:, b, :], pmax[:, b, :], -1.0, None, ALU.mult).then_inc(max_done, 1)

            def invert_sum(p, b):
                dve.wait_ge(exp_done, p.count(2, b + 1))
                nc.vector.reciprocal(rz[:, b, :], zsum[:, b, :]).then_inc(rz_done, 1)

            def first_residual(q):
                dve.wait_ge(xb_done, q.count(1, 1))
                for b in range(2):
                    dve.wait_ge(proj_done, q.count(2, b + 1))
                    nc.vector.tensor_tensor(xb[:, q.slot, b], B[:, b, :], xb[:, q.slot, b], ALU.add)\
                        .then_inc(x1_done, 1)

            def keep_yx_lo(q):
                dve.wait_ge(yhi_done, q.count(1, 1))
                splits_low(yx_lo[:], yx[:], yx_hi[:]).then_inc(ylo_done, 1)

            def demodulate(q):
                dve.wait_ge(l1_done, q.count(1, 1))
                for b in range(2):
                    last = nc.vector.tensor_tensor(
                        yx[:, :, b, :], A[:].rearrange("p a (c b l) -> p (a c) b l", c=2, b=2)[:, :, b, :],
                        dnorm[:, q.batch() + b, :].unsqueeze(2).to_broadcast([P, NC, P]), ALU.mult)
                last.then_inc(dn_done, 1)

            def keep_aT_lo(p):
                for b in range(2):
                    dve.wait_ge(ahi_done, p.count(2, b + 1))
                    for c in range(NC):
                        last = nc.vector.scalar_tensor_tensor(
                            out=aT_lo[:, b, c, :], in0=A[:, b, P * c:P * c + P],
                            scalar=vimgT[:, p.batch() + b, c:c + 1], in1=aT_hi[:, b, c, :].bitcast(F32),
                            op0=ALU.add, op1=ALU.subtract)
                    last.then_inc(alo_done, 1)

            keep_xT_lo(Pair(0, 0))
            dve.wait_ge(kbd_zero, 1)
            dve.wait_ge(image_kept, 2)
            keep_k(Pair(0, 0))
            keep_v(Pair(0, 0))

            def step(p, back, ahead):
                row_max(p, 0)
                if ahead:
                    keep_xT_lo(p.at(1))
                row_max(p, 1)
                if back:
                    first_residual(p.at(-1))
                    keep_yx_lo(p.at(-1))
                invert_sum(p, 0)
                if ahead:
                    keep_k(p.at(1))
                invert_sum(p, 1)
                if back:
                    demodulate(p.at(-1))
                if ahead:
                    keep_v(p.at(1))
                keep_aT_lo(p)

            run_pairs(dve, step)
            first_residual(LAST)
            keep_yx_lo(LAST)
            demodulate(LAST)

        @block.tensor
        def _(pe):
            def three_products(out_ap, lhs_rhs_pairs):
                n = len(lhs_rhs_pairs)
                for i, ((l_h, l_l), (r_h, r_l)) in enumerate(lhs_rhs_pairs):
                    nc.tensor.matmul(out_ap, l_h, r_h, start=(i == 0), stop=False)
                    nc.tensor.matmul(out_ap, l_h, r_l, start=False, stop=False)
                    last = nc.tensor.matmul(out_ap, l_l, r_h, start=False, stop=(i == n - 1))
                return last

            def transposes(u, blocks):
                if u >= 8:
                    pe.wait_ge(tr_kept, u - 7)
                for n, block_ap in enumerate(blocks):
                    last = nc.tensor.transpose(banks[u % 8][:, P * n:P * n + P], block_ap, ident[:])
                last.then_inc(tr_done, 1)

            pe.wait_ge(ident_ready, 2)
            pe.wait_ge(cond_loaded, 16)
            transposes(COND, [cond_nat[:, P * c:P * c + P] for c in range(NC)])
            by_chunk = cond_nat.rearrange("p (s c) -> p c s", c=NC)
            transposes(Y, [by_chunk[:, c, :] for c in range(NC)])
            pe.wait_ge(uk_loaded, 16)
            for n in range(NC):
                transposes(UK + n, [uk_nat[:, o, P * n:P * n + P] for o in range(NC)])
            pe.wait_ge(uv_loaded, 16)
            for n in range(NC):
                transposes(UV + n, [uv_nat[:, o, P * n:P * n + P] for o in range(NC)])
            pe.wait_ge(l_loaded, 16)
            l_by_chunk = l_nat.rearrange("p d (s c) -> p c d s", c=NC)
            for c in range(NC):
                transposes(L1 + c, [l_by_chunk[:, c, d, :] for d in range(NC)])
            pe.wait_ge(tr_kept, L1)
            for wT, bank in ((ukT, banks[6]), (uvT, banks[7])):
                for o in range(NC):
                    for n in range(NC):
                        last = nc.tensor.matmul(bank[:, P * o:P * o + P], wT[:, n, P * o:P * o + P], condT[:, n, :],
                                                start=(n == 0), stop=(n == NC - 1))
                last.then_inc(image_done, 1)
            for n in range(NC):
                last = nc.tensor.matmul(banks[0], condT[:, n, :], uvT[:, n, :], start=(n == 0), stop=(n == NC - 1))
            last.then_inc(image_done, 1)
            pe.wait_ge(tr_kept, TR)
            for d in range(NC):
                for c in range(NC):
                    last = nc.tensor.matmul(banks[1][:, P * d:P * d + P], w_sq[:, c, d, :], ysq[:, c, :],
                                            start=(c == 0), stop=(c == NC - 1))
            last.then_inc(dn_sum, 1)
            pe.wait_ge(l_lo_done, NC)
            pe.wait_ge(image_kept, 2)
            pe.wait_ge(vrow_ready, 2)
            pe.wait_ge(dn_step, 1)

            def transpose_x(p, back):
                pe.wait_ge(x_loaded[p.slot], p.dma())
                if back:
                    pe.wait_ge(alo_done, p.at(-2).count(2, 2))
                for b in range(2):
                    for c in range(NC):
                        last = nc.tensor.transpose(A[:, b, P * c:P * c + P], xin[:, p.slot, b, P * c:P * c + P],
                                                   ident[:])
                    last.then_inc(xt_done, 1)

            def columns(unit, c):
                return unit[:, c // 2, 256 * (c % 2):256 * (c % 2) + 256]

            def x_moving(n):
                return xT_hi[:, n].rearrange("p b t -> p (b t)"), xT_lo[:, n].rearrange("p b t -> p (b t)")

            def project_k(p):
                pe.wait_ge(xlo_done, p.count(1, 1))
                for c in range(NC):
                    w = slice(E + P * c, E + P * c + P)
                    last = three_products(columns(A, c), [((w_hi[:, n, w], w_lo[:, n, w]), x_moving(n))
                                                          for n in range(NC)])
                last.then_inc(k_done, 1)

            def project_q(p, back):
                if back:
                    pe.wait_ge(x1_done, p.at(-2).count(2, 2))
                for c in range(NC):
                    w = slice(P * c, P * c + P)
                    last = three_products(columns(B, c), [((w_hi[:, n, w], w_lo[:, n, w]), x_moving(n))
                                                          for n in range(NC)])
                    if c % 2:
                        last.then_inc(q_done, 1)

            def project_v(p):
                for b in range(2):
                    pe.wait_ge(q_kept, p.count(2, b + 1))
                    last = three_products(B[:, b, :], [((xT_hi[:, n, b, :], xT_lo[:, n, b, :]),
                                                        (w_hi[:, n, 2 * E:], w_lo[:, n, 2 * E:]))
                                                       for n in range(NC)])
                    last.then_inc(v_done, 1)

            def scores(p, back):
                pe.wait_ge(q_kept, p.count(2, 2))
                pe.wait_ge(k_kept, p.count(1, 1))
                for n in range(8):
                    b, c = n // 4, n % 4
                    if n >= 2:
                        pe.wait_ge(s_kept, p.count(8, n - 1))
                    elif back:
                        pe.wait_ge(pt_kept, p.at(-1).count(8, 6 + 2 * n))
                    moving = kbd[:, b, c].rearrange("p h k -> p (h k)")
                    for a in range(2):
                        last = nc.tensor.matmul(att[:, 2 * (n % 2) + a, 0:HALF], qT[:, c, P * b:P * b + P],
                                                moving[:, HALF * a:HALF * a + HALF], start=True, stop=True)
                    last.then_inc(s_done, 1)

            def attend(p):
                def transpose_p(n):
                    b, c = n // 4, n % 4
                    pe.wait_ge(norm_done, p.count(8, n + 1))
                    if n < 4:
                        pe.wait_ge(s_kept, p.count(8, 7 + n // 2))
                    else:
                        pe.wait_ge(pt_kept, p.count(8, n - 3))
                    for j in range(HC):
                        last = nc.tensor.transpose(att[:, n % 4, P * j:P * j + P], S[b][:, HC * c + j, 0:P], ident[:])
                    last.then_inc(pt_done, 1)

                transpose_p(0)
                transpose_p(1)
                pe.wait_ge(v_kept, p.count(2, 2))
                for n in range(8):
                    if n + 2 < 8:
                        transpose_p(n + 2)
                    b, c = n // 4, n % 4
                    pe.wait_ge(pt_kept, p.count(8, n + 1))
                    for j in range(HC):
                        h = HC * c + j
                        last = nc.tensor.matmul(A[HD * j:HD * j + HD, b, P * c:P * c + P],
                                                v[:, p.slot, b, HD * h:HD * h + HD], pT[:, n % 4, j, :],
                                                start=True, stop=True)
                    last.then_inc(av_done, 1)

            def project_out(q):
                for b in range(2):
                    pe.wait_ge(alo_done, q.count(2, b + 1))
                    last = three_products(B[:, b, :], [((aT_hi[:, b, n, :], aT_lo[:, b, n, :]),
                                                        (wp_hi[:, n, :], wp_lo[:, n, :])) for n in range(NC)])
                    last.then_inc(proj_done, 1)

            def modulated(q):
                pe.wait_ge(ylo_done, q.count(1, 1))
                for d in range(NC):
                    last = three_products(columns(A, d), [
                        ((l_hi[:, c, d, :], l_lo[:, c, d, :]),
                         (yx_hi[:, c].rearrange("p b l -> p (b l)"), yx_lo[:, c].rearrange("p b l -> p (b l)")))
                        for c in range(NC)])
                last.then_inc(l1_done, 1)

            transpose_x(Pair(0, 0), 0)
            pe.wait_ge(w_lo_done, NC)
            project_k(Pair(0, 0))
            project_q(Pair(0, 0), 0)
            project_v(Pair(0, 0))
            pe.wait_ge(w_lo_done, NC + 1)

            def step(p, back, ahead):
                scores(p, back)
                if ahead:
                    transpose_x(p.at(1), back)
                if back:
                    pe.wait_ge(v_kept, p.count(2, 2))
                    project_out(p.at(-1))
                if ahead:
                    project_k(p.at(1))
                    if not back:
                        pe.wait_ge(v_kept, p.count(2, 2))
                    project_q(p.at(1), back)
                if back:
                    if ahead:
                        pe.wait_ge(k_kept, p.at(1).count(1, 1))
                    modulated(p.at(-1))
                if ahead:
                    project_v(p.at(1))
                if back:
                    pe.wait_ge(dn_done, p.at(-1).count(1, 1))
                else:
                    pe.wait_ge(k_kept, p.at(1).count(1, 1))
                attend(p)

            run_pairs(pe, step)
            project_out(LAST)
            modulated(LAST)


_INS = ['x', 'cond_1024', 'mask_Bx1x1xS_ff0', 'L0_cond_c_attn_w', 'L0_cond_c_attn_b', 'L0_cond_c_proj_w',
        'L0_cond_c_proj_b', 'L0_cond_uk_w', 'L0_cond_uk_b', 'L0_cond_uv_w', 'L0_cond_uv_b', 'L1_cond_weight']


def kernel(**inputs):
    import numpy as _np
    import concourse.bacc as _bacc
    from concourse import mybir as _mybir
    from concourse.bass_utils import run_bass_kernel_spmd as _run

    nc = _bacc.Bacc("TRN2", target_bir_lowering=False, num_devices=1)
    arrays, args = {}, []
    for name in _INS:
        a = _np.ascontiguousarray(inputs[name])
        arrays[f"in_{name}"] = a
        args.append(nc.dram_tensor(f"in_{name}", a.shape, _mybir.dt.from_np(a.dtype), kind="ExternalInput").ap())
    args.append(nc.dram_tensor("out_0", (NB, P, E), _mybir.dt.float32, kind="ExternalOutput").ap())
    build(nc, *args)
    r = _run(nc, [arrays], core_ids=[0])
    return r.results[0]["out_0"]
```

```python
from contextlib import ExitStack

import concourse.bass as bass
from concourse import mybir

ALU = mybir.AluOpType
ACT = mybir.ActivationFunctionType
F32 = mybir.dt.float32
F32R = mybir.dt.float32r

P = 128
NB = 128
PAIRS = NB // 2
E = 512
NC = E // P
HD = 32
HC = P // HD
H = E // HD
KEYS = P + 1
IMG = P

KPAD = KEYS + 1
MASK_OUT = -10000.0
LOWEST = -3.4e38
QSCALE = float(HD) ** -0.5
WSCALE = float(E) ** -0.5
EPS = 1e-8


class Pair:

    def __init__(self, t, k):
        self.t, self.k = t, k

    def at(self, d):
        return Pair(self.t, self.k + d)

    @property
    def slot(self):
        return self.k % 2

    def count(self, per, n):
        return self.t * (2 * per) + (self.k * per + n)

    def dma(self, n=1):
        return self.t * 16 + (self.k // 2 + n) * 16

    def batch(self):
        return self.t * 4 + self.k * 2


def build(nc, x, cond, mask, wqkv, bqkv, wproj, bproj, uk_w, uk_b, uv_w, uv_b, l1w, out):
    x_v = x.rearrange("b s e -> s b e")
    out_v = out.rearrange("b s e -> s b e")
    vrow_dram = nc.dram_tensor("v_rows", [NB, E], F32, kind="Internal").ap()

    with ExitStack() as ctx:
        def sb(name, shape, dt=F32):
            return ctx.enter_context(nc.sbuf_tensor(name, shape, dt))

        def sem(name):
            return ctx.enter_context(nc.semaphore(name))

        w_hi = sb("w_hi", [P, NC, 3 * E], F32R)
        w_lo = sb("w_lo", [P, NC, 3 * E], F32R)
        wp_hi = sb("wp_hi", [P, NC, E], F32R)
        wp_lo = sb("wp_lo", [P, NC, E], F32R)
        l_hi = sb("l_hi", [P, NC, NC, P], F32R)
        l_lo = sb("l_lo", [P, NC, NC, P], F32R)
        ident0 = sb("ident0", [P, P])
        ident = sb("ident", [P, P])
        qbias = sb("qbias", [P, NC])
        kbias = sb("kbias", [P, NC])
        ukbias = sb("ukbias", [P, NC])
        uvbias = sb("uvbias", [P, NC])
        pbias = sb("pbias", [P, E])
        kimgT = sb("kimgT", [P, NB, NC])
        vimgT = sb("vimgT", [P, NB, NC])
        ysc = sb("ysc", [P, NB, NC])
        dnorm = sb("dnorm", [P, NB, NC])
        vrow = sb("vrow", [P, 2, E])
        xin = sb("xin", [P, 2, 2, E])
        xb = sb("xb", [P, 2, 2, E])
        xT_hi = sb("xT_hi", [P, NC, 2, P], F32R)
        xT_lo = sb("xT_lo", [P, NC, 2, P], F32R)
        kc = sb("kc", [P, 2, NC, 2, KPAD])
        q_st = sb("q_st", [P, 2, NC, 2, P], F32R)
        k_hi = sb("k_hi", [P, 2, 2, NC, 2, KPAD], F32R)
        k_lo = sb("k_lo", [P, 2, 2, NC, 2, KPAD], F32R)
        cond_st = sb("cond_st", [P, 2, E])
        v = sb("v", [P, 2, E])
        S = [sb(f"S{b}", [P, H, KEYS]) for b in range(2)]
        pT = sb("pT", [P, 4, HC, P])
        aT_hi = sb("aT_hi", [P, 2, NC, P], F32R)
        aT_lo = sb("aT_lo", [P, 2, NC, P], F32R)
        yx = sb("yx", [P, NC, 2, P])
        yx_hi = sb("yx_hi", [P, NC, 2, P], F32R)
        yx_lo = sb("yx_lo", [P, NC, 2, P], F32R)
        maskb = sb("maskb", [P, 2, 2, KEYS])
        nmax = sb("nmax", [P, 2, H])
        pmax = sb("pmax", [P, 2, H])
        zsum = sb("zsum", [P, 2, H])
        rz = sb("rz", [P, 2, H])

        kc_hi, kc_lo = kc[:, 0], kc[:, 1]
        qc_hi, qc_lo = (t[:].rearrange("p b c q -> p (b c q)").rearrange("p (c q) -> p c q", c=NC)
                        for t in (aT_hi, aT_lo))

        att = ctx.enter_context(nc.psum_tensor("att", [P, 4, 512], F32))
        A = ctx.enter_context(nc.psum_tensor("A", [P, 2, 512], F32))
        B = ctx.enter_context(nc.psum_tensor("B", [P, 2, 512], F32))

        def rows_of(ap):
            return ap.rearrange("p (o i) -> p o i", o=NC)

        flat_S = [s[:].rearrange("p h k -> p (h k)") for s in S]
        flat_xb = xb[:].rearrange("p a b e -> p (a b e)")
        w_stage = [ap[:, 0:3 * E] for ap in (flat_S[0], flat_S[1], flat_xb, pT[:].rearrange("p n h q -> p (n h q)"))]
        uk_nat = rows_of(kc[:].rearrange("p n c b k -> p (n c b k)")[:, 0:NC * E])
        uv_nat = rows_of(flat_S[1][:, 0:NC * E])
        wp_stage = flat_xb
        l_nat = rows_of(flat_S[0][:, 0:NC * E])
        w_sq = flat_S[1][:, 0:NC * E].rearrange("p (c d s) -> p c d s", c=NC, d=NC)
        uT = [v[:, 0, :], v[:, 1, :], xin[:, 1, 0, :], xin[:, 1, 1, :]]
        cond_nat, condT = cond_st[:, 0], cond_st[:, 1].rearrange("p (c b) -> p c b", c=NC)
        yx_flat = yx[:].rearrange("p c b t -> p (c b t)")
        uvb_bc, ysq = yx_flat[:, 0:E], yx_flat[:, E:2 * E].rearrange("p (c b) -> p c b", c=NC)
        vb_bc, vrow_st = vrow[:, 1, :], vrow[:, 0, :]
        dn_u, dn_r, dn_t = (ap.rearrange("p (d b) -> p d b", d=NC) for ap in (uvb_bc, cond_st[:, 0], cond_st[:, 1]))

        w_loaded = [sem(f"w_loaded{n}") for n in range(NC)]
        cond_loaded, uk_loaded, uv_loaded = sem("cond_loaded"), sem("uk_loaded"), sem("uv_loaded")
        l_loaded, wp_loaded, bias_loaded = sem("l_loaded"), sem("wp_loaded"), sem("bias_loaded")
        ident_ready, mask_zero, k_zero = sem("ident_ready"), sem("mask_zero"), sem("k_zero")
        w_hi_done, w_lo_done = sem("w_hi_done"), sem("w_lo_done")
        unit_done = sem("unit_done")
        unit_kept = sem("unit_kept")
        l_lo_done = sem("l_lo_done")
        vrow_ready, vrow_stored = sem("vrow_ready"), sem("vrow_stored")
        dn_step, dn_root = sem("dn_step"), sem("dn_root")

        x_loaded = [sem(f"x_loaded{n}") for n in range(2)]
        mask_loaded = [sem(f"mask_loaded{n}") for n in range(2)]
        stored = [sem(f"stored{n}") for n in range(2)]
        vrow_loaded = sem("vrow_loaded")
        xt_done = sem("xt_done")
        xhi_done = sem("xhi_done")
        xlo_done = sem("xlo_done")
        k_done, q_done, v_done = sem("k_done"), sem("q_done"), sem("v_done")
        khi_done, qhi_done, v_kept = sem("khi_done"), sem("qhi_done"), sem("v_kept")
        s_done, s_kept = sem("s_done"), sem("s_kept")
        sel_done = sem("sel_done")
        klo_done, qlo_done = sem("klo_done"), sem("qlo_done")
        k_placed, q_placed = sem("k_placed"), sem("q_placed")
        sel_seen, s_seen = sem("sel_seen"), sem("s_seen")
        rowmax_done, max_done = sem("rowmax_done"), sem("max_done")
        exp_done = sem("exp_done")
        rz_done = sem("rz_done")
        norm_done = sem("norm_done")
        pt_done, pt_kept = sem("pt_done"), sem("pt_kept")
        av_done = sem("av_done")
        ahi_done, alo_done = sem("ahi_done"), sem("alo_done")
        proj_done = sem("proj_done")
        xb_done = sem("xb_done")
        x1_done = sem("x1_done")
        yx_done = sem("yx_done")
        yhi_done, ylo_done = sem("yhi_done"), sem("ylo_done")
        l1_done = sem("l1_done")
        dn_done = sem("dn_done")
        out_done = sem("out_done")

        block = ctx.enter_context(nc.Block())

        def columns(unit, c):
            return unit[:, c // 2, 256 * (c % 2):256 * (c % 2) + 256]

        def run_pairs(eng, step):
            step(Pair(0, 0), 0, 2)
            step(Pair(0, 1), 1, 2)
            with eng.Fori(0, PAIRS // 2 - 2) as t:
                for k in (2, 3):
                    step(Pair(t, k), 2, 2)
            step(Pair(0, PAIRS - 2), 2, 1)
            step(Pair(0, PAIRS - 1), 2, 0)

        LAST = Pair(0, PAIRS - 1)

        COND, Y, UK, KIMG, UV, VIMG, VROW, L1, DN = 0, 1, 2, 6, 7, 11, 12, 13, 17

        def bank(u):
            return att[:, u % 4, :]

        def chunked(u):
            return bank(u).rearrange("p (c n) -> p c n", c=NC)

        @block.sync
        def _(sp):
            def load_x(p):
                sp.dma_start(xin[:, p.slot], x_v[:, bass.ds(p.batch(), 2), :]).then_inc(x_loaded[p.slot], 16)

            def load_mask(p):
                rows = mask[bass.ds(p.batch(), 2), 0, 0, :].partition_broadcast(P)
                sp.dma_start(maskb[:, p.slot, :, 0:P], rows).then_inc(mask_loaded[p.slot], 16)

            def place_k(p):
                for done, src, dst in ((khi_done, kc_hi, k_hi), (klo_done, kc_lo, k_lo)):
                    sp.wait_ge(done, p.count(1, 1))
                    flat = src.rearrange("p c b k -> p (c b k)")
                    for a in range(2):
                        for copy in range(2):
                            r = 2 * HD * copy + HD * a
                            to = dst[r:r + HD, :, a].bitcast(F32).rearrange("p s c b k -> p s (c b k)")
                            for s in range(2):
                                sp.dma_start(to[:, s], flat[64 * s + HD * a:64 * s + HD * a + HD]).then_inc(k_placed, 16)

            def place_q(p):
                sp.wait_ge(qlo_done, p.count(2, 2))
                for part, src in enumerate((qc_hi, qc_lo)):
                    for s in range(2):
                        to = q_st[64 * part:64 * part + 64, s].bitcast(F32).rearrange("p c b q -> p (c b q)")
                        sp.dma_start(to, src[64 * s:64 * s + 64].bitcast(F32).rearrange("p c q -> p (c q)"))\
                            .then_inc(q_placed, 16)

            def load_vrow(p):
                rows = vrow_dram[bass.ds(p.batch(), 2), :].partition_broadcast(P)
                sp.dma_start(vrow[:], rows).then_inc(vrow_loaded, 16)

            w_v = wqkv.rearrange("(c p) n -> p c n", p=P)
            sp.dma_start(cond_nat, cond).then_inc(cond_loaded, 16)
            sp.dma_start(uk_nat, uk_w.rearrange("(o p) i -> p o i", p=P)).then_inc(uk_loaded, 16)
            load_x(Pair(0, 0))
            for c in range(NC):
                sp.dma_start(w_stage[c], w_v[:, c, :]).then_inc(w_loaded[c], 16)
                if c == 0:
                    for dst, src in ((qbias, bqkv[0:E]), (kbias, bqkv[E:2 * E]), (ukbias, uk_b), (uvbias, uv_b)):
                        sp.dma_start(dst[:], src.rearrange("(c p) -> p c", p=P),
                                     allow_slow_non_contiguous=True).then_inc(bias_loaded, 16)
                    for dst, src in ((pbias[:], bproj), (vb_bc, bqkv[2 * E:3 * E]), (uvb_bc, uv_b)):
                        sp.dma_start(dst, src.partition_broadcast(P)).then_inc(bias_loaded, 16)
            sp.wait_ge(w_hi_done, 2)
            sp.wait_ge(w_lo_done, 2)
            sp.dma_start(uv_nat, uv_w.rearrange("(o p) i -> p o i", p=P)).then_inc(uv_loaded, 16)
            sp.dma_start(l_nat, l1w[0, :, :, 0].rearrange("(s d) i -> s d i", d=NC)).then_inc(l_loaded, 16)
            sp.wait_ge(w_hi_done, 3)
            sp.wait_ge(w_lo_done, 3)
            sp.dma_start(rows_of(wp_stage), wproj.rearrange("(c p) n -> p c n", p=P)).then_inc(wp_loaded, 16)
            sp.wait_ge(mask_zero, 1)
            load_mask(Pair(0, 0))
            sp.wait_ge(k_zero, 3)
            place_k(Pair(0, 0))
            place_q(Pair(0, 0))
            sp.wait_ge(vrow_ready, 2)
            sp.dma_start(vrow_dram, vrow_st).then_inc(vrow_stored, 16)
            sp.wait_ge(unit_done, VROW + 1)
            load_x(Pair(0, 1))
            sp.wait_ge(vrow_stored, 16)
            load_vrow(Pair(0, 0))

            def store(q):
                sp.wait_ge(out_done, q.count(1, 1))
                sp.dma_start(out_v[:, bass.ds(q.batch(), 2), :], xb[:, q.slot]).then_inc(stored[q.slot], 16)

            def step(p, back, ahead):
                if ahead:
                    if back:
                        sp.wait_ge(max_done, p.at(-1).count(2, 2))
                    load_mask(p.at(1))
                    sp.wait_ge(v_kept, p.count(2, 2))
                    load_vrow(p.at(1))
                    place_k(p.at(1))
                    place_q(p.at(1))
                if ahead > 1:
                    sp.wait_ge(xb_done, p.count(1, 1))
                    load_x(p.at(2))
                if back:
                    store(p.at(-1))

            run_pairs(sp, step)
            store(LAST)
            for n in range(2):
                sp.wait_ge(stored[n], 16 * (PAIRS // 2))

        @block.gpsimd
        def _(pool):
            nc.gpsimd.memset(ident0[:], 0.0).then_inc(ident_ready, 1)
            pool.wait_ge(ident_ready, 1)
            nc.gpsimd.affine_select(out=ident[:], in_=ident0[:], compare_op=ALU.not_equal, fill=1.0, base=0,
                                    pattern=[[-1, P]], channel_multiplier=1).then_inc(ident_ready, 1)
            nc.gpsimd.memset(maskb[:, :, :, IMG:KEYS], 0.0).then_inc(mask_zero, 1)
            nc.gpsimd.memset(k_hi[:].bitcast(F32), 0.0).then_inc(k_zero, 1)
            nc.gpsimd.memset(k_lo[:].bitcast(F32), 0.0).then_inc(k_zero, 1)
            pool.wait_ge(unit_done, UK + NC)
            nc.gpsimd.memset(kc[:, :, :, :, KEYS:KPAD], 0.0).then_inc(k_zero, 1)

            mask_out = pool.to_reg(MASK_OUT)

            def scale_y(q, b):
                pool.wait_ge(x1_done, q.count(2, b + 1))
                nc.gpsimd.tensor_tensor(
                    yx[:, :, b, :], xb[:, q.slot, b].rearrange("p (c l) -> p c l", c=NC),
                    ysc[:, q.batch() + b, :].unsqueeze(2).to_broadcast([P, NC, P]),
                    ALU.mult).then_inc(yx_done, 1)

            def normalize(p, b):
                pool.wait_ge(rz_done, p.count(2, b + 1))
                for c in range(NC):
                    heads = slice(HC * c, HC * c + HC)
                    s = S[b][:, heads, 0:P]
                    nc.gpsimd.tensor_tensor(s, s, rz[:, b, heads].unsqueeze(2).to_broadcast([P, HC, P]),
                                            ALU.mult).then_inc(norm_done, 1)

            def add_bias(p, back):
                pool.wait_ge(x_loaded[p.slot], p.dma())
                if back == 0:
                    pool.wait_ge(bias_loaded, 16 * 7)
                    pool.wait_ge(w_hi_done, NC + 1)
                    pool.wait_ge(w_lo_done, NC + 1)
                if back == 2:
                    pool.wait_ge(stored[p.slot], p.at(-2).dma())
                nc.gpsimd.tensor_tensor(xb[:, p.slot], xin[:, p.slot],
                                        pbias[:].unsqueeze(1).to_broadcast([P, 2, E]), ALU.add).then_inc(xb_done, 1)

            def add_out(q):
                pool.wait_ge(dn_done, q.count(2, 2))
                o = xb[:, q.slot].rearrange("p b (c l) -> p b c l", c=NC)
                nc.gpsimd.tensor_tensor(o, o, yx[:].rearrange("p c b l -> p b c l"), ALU.add).then_inc(out_done, 1)

            def step(p, back, ahead):
                for b in range(2):
                    for g in range(2):
                        pool.wait_ge(s_kept, p.count(8, 4 * b + 2 * g + 2))
                        pool.sem_inc(s_seen, 1)
                        s = S[b][:, 8 * g:8 * g + 8, 0:P]
                        nc.gpsimd.affine_select(out=s, in_=s, compare_op=ALU.is_ge, fill=mask_out, base=0,
                                                pattern=[[0, 8], [-1, P]], channel_multiplier=1)\
                            .then_inc(sel_done, 1)
                add_bias(p, back)
                if back:
                    scale_y(p.at(-1), 0)
                normalize(p, 0)
                if back:
                    scale_y(p.at(-1), 1)
                normalize(p, 1)
                if back:
                    add_out(p.at(-1))

            run_pairs(pool, step)
            pool.wait_ge(out_done, LAST.at(-1).count(1, 1))
            scale_y(LAST, 0)
            scale_y(LAST, 1)
            add_out(LAST)

        @block.scalar
        def _(act):
            def keep_xT_hi(p):
                act.wait_ge(xt_done, p.count(2, 2))
                nc.scalar.activation(xT_hi[:].rearrange("p e b t -> p b e t"),
                                     A[:].rearrange("p b (e t) -> p b e t", e=NC), ACT.Copy).then_inc(xhi_done, 1)

            def keep_q_hi(p):
                for c in range(NC):
                    if c % 2 == 0:
                        act.wait_ge(q_done, p.count(2, c // 2 + 1))
                    last = nc.scalar.activation(qc_hi[:, c, :], columns(B, c), ACT.Identity, bias=qbias[:, c:c + 1])
                    if c % 2:
                        last.then_inc(qhi_done, 1)

            def keep_k_hi(p):
                act.wait_ge(k_done, p.count(1, 1))
                for c in range(NC):
                    nc.scalar.activation(kc_hi[:, c, :, 0:P].bitcast(F32R),
                                         columns(A, c).rearrange("p (b t) -> p b t", b=2), ACT.Identity,
                                         bias=kbias[:, c:c + 1])
                nc.scalar.activation(kc_hi[:, :, :, IMG].bitcast(F32R).rearrange("p c b -> p b c"),
                                     kimgT[:, bass.ds(p.batch(), 2), :], ACT.Copy).then_inc(khi_done, 1)

            def exps(p, b, heads):
                if heads[0] == 0:
                    act.wait_ge(max_done, p.count(2, b + 1))
                for h in heads:
                    last = nc.scalar.activation(S[b][:, h, :], S[b][:, h, :], ACT.Exp, bias=nmax[:, b, h:h + 1],
                                                accum_out=zsum[:, b, h:h + 1])
                if h == H - 1:
                    last.then_inc(exp_done, 1)

            def keep_yx_hi(q, b):
                act.wait_ge(yx_done, q.count(2, b + 1))
                nc.scalar.activation(yx_hi[:, :, b], yx[:, :, b], ACT.Copy).then_inc(yhi_done, 1)

            def keep_unit(u, out_ap, in_ap):
                act.wait_ge(unit_done, u + 1)
                return nc.scalar.activation(out_ap, in_ap, ACT.Copy)

            def keep_image(u, dst, bias):
                act.wait_ge(unit_done, u + 1)
                for c in range(NC):
                    last = nc.scalar.activation(dst[:, :, c], bank(u)[:, P * c:P * c + P], ACT.Identity,
                                                bias=bias[:, c:c + 1])
                last.then_inc(unit_kept, 1)

            keep_unit(COND, condT, chunked(COND)).then_inc(unit_kept, 1)
            keep_unit(Y, ysc[:].rearrange("p b c -> p c b"), chunked(Y))
            act.wait_ge(bias_loaded, 16 * 7)
            nc.scalar.activation(ysq, chunked(Y), ACT.Square).then_inc(unit_kept, 1)
            for n in range(NC):
                keep_unit(UK + n, uT[n], bank(UK + n)).then_inc(unit_kept, 1)
            keep_image(KIMG, kimgT, ukbias)
            keep_xT_hi(Pair(0, 0))
            for c in range(NC):
                act.wait_ge(w_loaded[c], 16)
                nc.scalar.activation(w_hi[:, c, :], w_stage[c], ACT.Copy).then_inc(w_hi_done, 1)
            keep_k_hi(Pair(0, 0))
            keep_q_hi(Pair(0, 0))
            for n in range(NC):
                keep_unit(UV + n, uT[n], bank(UV + n)).then_inc(unit_kept, 1)
            keep_image(VIMG, vimgT, uvbias)
            act.wait_ge(w_lo_done, 2)
            for c in range(NC):
                keep_unit(L1 + c, l_hi[:, c].rearrange("p d s -> p (d s)"), bank(L1 + c))
                nc.scalar.activation(w_sq[:, c].rearrange("p d s -> p (d s)"), bank(L1 + c),
                                     ACT.Square).then_inc(unit_kept, 1)
            act.wait_ge(wp_loaded, 16)
            nc.scalar.activation(wp_hi[:].rearrange("p c n -> p (c n)"), wp_stage, ACT.Copy).then_inc(w_hi_done, 1)
            act.wait_ge(dn_step, 1)
            nc.scalar.activation(dn_r, dn_u, ACT.Sqrt).then_inc(dn_root, 1)

            def step(p, back, ahead):
                for n in range(8):
                    act.wait_ge(s_done, p.count(8, n + 1))
                    c = n % 4
                    scores = att[:, 2 * (n % 2):2 * (n % 2) + 2, 0:2 * KPAD].rearrange("p s (a k) -> p s a k", a=2)
                    nc.scalar.activation(S[n // 4][:, HC * c:HC * c + HC, :].rearrange("p (s a) k -> p s a k", a=2),
                                         scores[:, :, :, 0:KEYS], ACT.Copy, scale=QSCALE).then_inc(s_kept, 1)
                    if n == 0 and back:
                        keep_aT_hi(p.at(-1), 1)
                if ahead:
                    keep_xT_hi(p.at(1))
                exps(p, 0, range(H))
                exps(p, 1, range(0, 4))
                if ahead:
                    keep_k_hi(p.at(1))
                if back:
                    keep_yx_hi(p.at(-1), 0)
                exps(p, 1, range(4, 10))
                if back:
                    keep_yx_hi(p.at(-1), 1)
                exps(p, 1, range(10, H))
                if ahead:
                    keep_q_hi(p.at(1))
                for n in range(8):
                    act.wait_ge(pt_done, p.count(8, n + 1))
                    if n >= 4 or back:
                        act.wait_ge(av_done, p.count(8, n - 3))
                    nc.scalar.activation(pT[:, n % 4].rearrange("p h q -> p (h q)"), att[:, n % 4, :],
                                         ACT.Copy).then_inc(pt_kept, 1)
                if ahead:
                    act.wait_ge(q_placed, p.at(1).count(64, 64))
                keep_aT_hi(p, 0)

            def keep_aT_hi(p, b):
                act.wait_ge(av_done, p.count(8, 4 * b + 4))
                for c in range(NC):
                    last = nc.scalar.activation(aT_hi[:, b, c, :], A[:, b, P * c:P * c + P], ACT.Identity,
                                                bias=vimgT[:, p.batch() + b, c:c + 1])
                last.then_inc(ahi_done, 1)

            run_pairs(act, step)
            keep_aT_hi(LAST, 1)
            keep_yx_hi(LAST, 0)
            keep_yx_hi(LAST, 1)

        @block.vector
        def _(dve):
            def splits_low(out_ap, in_ap, hi_ap):
                return nc.vector.tensor_tensor(out_ap, in_ap, hi_ap.bitcast(F32), ALU.subtract)

            def keep_xT_lo(p):
                dve.wait_ge(xhi_done, p.count(1, 1))
                splits_low(xT_lo[:].rearrange("p e b t -> p b e t"), A[:].rearrange("p b (e t) -> p b e t", e=NC),
                           xT_hi[:].rearrange("p e b t -> p b e t")).then_inc(xlo_done, 1)

            def keep_k_lo(p):
                dve.wait_ge(khi_done, p.count(1, 1))
                for c in range(NC):
                    nc.vector.scalar_tensor_tensor(
                        out=kc_lo[:, c, :, 0:P].bitcast(F32R), in0=columns(A, c).rearrange("p (b t) -> p b t", b=2),
                        scalar=kbias[:, c:c + 1], in1=kc_hi[:, c, :, 0:P], op0=ALU.add, op1=ALU.subtract)
                nc.vector.tensor_tensor(
                    kc_lo[:, :, :, IMG].bitcast(F32R).rearrange("p c b -> p b c"),
                    kimgT[:, bass.ds(p.batch(), 2), :], kc_hi[:, :, :, IMG].rearrange("p c b -> p b c"),
                    ALU.subtract).then_inc(klo_done, 1)

            def keep_q_lo(p):
                for c in range(NC):
                    if c % 2 == 0:
                        dve.wait_ge(qhi_done, p.count(2, c // 2 + 1))
                    last = nc.vector.scalar_tensor_tensor(
                        out=qc_lo[:, c, :], in0=columns(B, c), scalar=qbias[:, c:c + 1],
                        in1=qc_hi[:, c, :].bitcast(F32), op0=ALU.add, op1=ALU.subtract)
                    if c % 2:
                        last.then_inc(qlo_done, 1)

            def keep_v(p, b):
                dve.wait_ge(vrow_loaded, p.count(16, 16))
                dve.wait_ge(v_done, p.count(2, b + 1))
                nc.vector.tensor_tensor(v[:, b, :], B[:, b, :], vrow[:, b, :], ALU.add).then_inc(v_kept, 1)

            def row_max(p, b):
                if b == 0:
                    dve.wait_ge(mask_loaded[p.slot], p.dma())
                for h in range(H):
                    if h % 8 == 0:
                        dve.wait_ge(sel_done, p.count(4, 2 * b + h // 8 + 1))
                        dve.sem_inc(sel_seen, 1)
                    last = nc.vector.tensor_tensor_reduce(
                        out=S[b][:, h, :], in0=S[b][:, h, :], in1=maskb[:, p.slot, b, :], scale=1.0, scalar=LOWEST,
                        op0=ALU.add, op1=ALU.max, accum_out=pmax[:, b, h:h + 1])
                last.then_inc(rowmax_done, 1)
                dve.wait_ge(rowmax_done, p.count(2, b + 1))
                nc.vector.tensor_scalar(nmax[:, b, :], pmax[:, b, :], -1.0, None, ALU.mult).then_inc(max_done, 1)

            def invert_sum(p, b):
                dve.wait_ge(exp_done, p.count(2, b + 1))
                nc.vector.reciprocal(rz[:, b, :], zsum[:, b, :]).then_inc(rz_done, 1)

            def first_residual(q, b):
                if b == 0:
                    dve.wait_ge(xb_done, q.count(1, 1))
                dve.wait_ge(proj_done, q.count(2, b + 1))
                nc.vector.tensor_tensor(xb[:, q.slot, b], B[:, b, :], xb[:, q.slot, b], ALU.add).then_inc(x1_done, 1)

            def keep_yx_lo(q, b):
                dve.wait_ge(yhi_done, q.count(2, b + 1))
                splits_low(yx_lo[:, :, b], yx[:, :, b], yx_hi[:, :, b]).then_inc(ylo_done, 1)

            def demodulate(q):
                for a in range(2):
                    dve.wait_ge(l1_done, q.count(2, a + 1))
                    norm = dnorm[:, bass.ds(q.batch(), 2), 2 * a:2 * a + 2].rearrange("p b d -> p d b")
                    nc.vector.tensor_tensor(
                        yx[:, 2 * a:2 * a + 2], A[:, a].rearrange("p (d b l) -> p d b l", d=2, b=2),
                        norm.unsqueeze(3).to_broadcast([P, 2, 2, P]), ALU.mult).then_inc(dn_done, 1)

            def keep_aT_lo(p, b):
                dve.wait_ge(ahi_done, p.count(2, b + 1))
                for c in range(NC):
                    last = nc.vector.scalar_tensor_tensor(
                        out=aT_lo[:, b, c, :], in0=A[:, b, P * c:P * c + P],
                        scalar=vimgT[:, p.batch() + b, c:c + 1], in1=aT_hi[:, b, c, :].bitcast(F32),
                        op0=ALU.add, op1=ALU.subtract)
                last.then_inc(alo_done, 1)

            dve.wait_ge(bias_loaded, 16 * 7)
            nc.vector.tensor_tensor(vb_bc, vb_bc, uvb_bc, ALU.subtract).then_inc(vrow_ready, 1)
            keep_xT_lo(Pair(0, 0))
            for c in range(NC):
                dve.wait_ge(w_hi_done, c + 1)
                splits_low(w_lo[:, c, :], w_stage[c], w_hi[:, c, :]).then_inc(w_lo_done, 1)
            keep_k_lo(Pair(0, 0))
            keep_q_lo(Pair(0, 0))
            dve.wait_ge(unit_done, VROW + 1)
            dve.wait_ge(vrow_ready, 1)
            nc.vector.tensor_tensor(vrow_st, vb_bc, bank(VROW), ALU.subtract).then_inc(vrow_ready, 1)
            for c in range(NC):
                dve.wait_ge(unit_kept, L1 + c)
                splits_low(l_lo[:, c].rearrange("p d s -> p (d s)"), bank(L1 + c),
                           l_hi[:, c].rearrange("p d s -> p (d s)")).then_inc(l_lo_done, 1)
            dve.wait_ge(w_hi_done, NC + 1)
            splits_low(wp_lo[:].rearrange("p c n -> p (c n)"), wp_stage,
                       wp_hi[:].rearrange("p c n -> p (c n)")).then_inc(w_lo_done, 1)
            dve.wait_ge(unit_done, DN + 1)
            nc.vector.tensor_scalar(dn_u, chunked(DN), WSCALE * WSCALE, EPS, ALU.mult, ALU.add).then_inc(dn_step, 1)
            dve.wait_ge(dn_root, 1)
            nc.vector.reciprocal(dn_t, dn_r).then_inc(dn_step, 1)
            dve.wait_ge(dn_step, 2)
            nc.vector.tensor_tensor(dn_r, dn_t, dn_t, ALU.mult).then_inc(dn_step, 1)
            dve.wait_ge(dn_step, 3)
            nc.vector.tensor_tensor(dn_r, dn_r, dn_u, ALU.mult).then_inc(dn_step, 1)
            dve.wait_ge(dn_step, 4)
            nc.vector.tensor_scalar(dn_r, dn_r, -0.5, 1.5, ALU.mult, ALU.add).then_inc(dn_step, 1)
            dve.wait_ge(dn_step, 5)
            nc.vector.scalar_tensor_tensor(out=dnorm[:].rearrange("p b d -> p d b"), in0=dn_t, scalar=WSCALE,
                                           in1=dn_r, op0=ALU.mult, op1=ALU.mult).then_inc(dn_step, 1)
            dve.wait_ge(dn_step, 6)

            def step(p, back, ahead):
                keep_v(p, 0)
                row_max(p, 0)
                keep_v(p, 1)
                if ahead:
                    keep_xT_lo(p.at(1))
                row_max(p, 1)
                if back:
                    first_residual(p.at(-1), 0)
                invert_sum(p, 0)
                if back:
                    first_residual(p.at(-1), 1)
                if ahead:
                    keep_k_lo(p.at(1))
                if back:
                    keep_yx_lo(p.at(-1), 0)
                    keep_yx_lo(p.at(-1), 1)
                invert_sum(p, 1)
                if ahead:
                    keep_q_lo(p.at(1))
                if back:
                    demodulate(p.at(-1))
                keep_aT_lo(p, 0)
                keep_aT_lo(p, 1)

            run_pairs(dve, step)
            first_residual(LAST, 0)
            first_residual(LAST, 1)
            keep_yx_lo(LAST, 0)
            keep_yx_lo(LAST, 1)
            demodulate(LAST)

        @block.tensor
        def _(pe):
            def three_products(out_ap, lhs_rhs_pairs):
                n = len(lhs_rhs_pairs)
                for i, ((l_h, l_l), (r_h, r_l)) in enumerate(lhs_rhs_pairs):
                    nc.tensor.matmul(out_ap, l_h, r_h, start=(i == 0), stop=False)
                    nc.tensor.matmul(out_ap, l_h, r_l, start=False, stop=False)
                    last = nc.tensor.matmul(out_ap, l_l, r_h, start=False, stop=(i == n - 1))
                return last

            def transpose_x(p, back):
                pe.wait_ge(x_loaded[p.slot], p.dma())
                if back:
                    pe.wait_ge(alo_done, p.at(-2).count(2, 2))
                for b in range(2):
                    for c in range(NC):
                        last = nc.tensor.transpose(A[:, b, P * c:P * c + P], xin[:, p.slot, b, P * c:P * c + P],
                                                   ident[:])
                    last.then_inc(xt_done, 1)

            def x_moving(n):
                return xT_hi[:, n].rearrange("p b t -> p (b t)"), xT_lo[:, n].rearrange("p b t -> p (b t)")

            def project_k(p):
                pe.wait_ge(xlo_done, p.count(1, 1))
                for c in range(NC):
                    w = slice(E + P * c, E + P * c + P)
                    last = three_products(columns(A, c), [((w_hi[:, n, w], w_lo[:, n, w]), x_moving(n))
                                                          for n in range(NC)])
                last.then_inc(k_done, 1)

            def project_q(p, back):
                for c in range(NC):
                    if back and c % 2 == 0:
                        pe.wait_ge(x1_done, p.at(-2).count(2, c // 2 + 1))
                    w = slice(P * c, P * c + P)
                    last = three_products(columns(B, c), [((w_hi[:, n, w], w_lo[:, n, w]), x_moving(n))
                                                          for n in range(NC)])
                    if c % 2:
                        last.then_inc(q_done, 1)

            def project_v(p):
                for b in range(2):
                    pe.wait_ge(qlo_done, p.count(2, b + 1))
                    for n in range(NC):
                        x_h, x_l, w_h, w_l = xT_hi[:, n, b, :], xT_lo[:, n, b, :], w_hi[:, n, 2 * E:], w_lo[:, n, 2 * E:]
                        for m, (left, right) in enumerate(((x_h, w_h), (x_h, w_l), (x_l, w_h))):
                            last = nc.tensor.matmul(B[:, b, :], left, right, start=(n == m == 0),
                                                    stop=(n == NC - 1 and m == 2))
                            if n == NC - 1 and m == 2:
                                last.then_inc(v_done, 1)
                            yield

            def scores_and_v(p, back):
                v_steps = project_v(p)
                pe.wait_ge(q_placed, p.count(64, 64))
                pe.wait_ge(k_placed, p.count(256, 256))
                for n in range(8):
                    b, c = n // 4, n % 4
                    if n >= 2:
                        pe.wait_ge(s_kept, p.count(8, n - 1))
                    elif back:
                        pe.wait_ge(pt_kept, p.at(-1).count(8, 6 + 2 * n))
                    for s in range(2):
                        q = q_st[:, s, c, b, :]
                        to = att[:, 2 * (n % 2) + s, 0:2 * KPAD]
                        nc.tensor.matmul(to, q, k_hi[:, s, :, c, b, :], start=True, stop=False)
                        last = nc.tensor.matmul(to, q, k_lo[:, s, :, c, b, :], start=False, stop=True)
                    last.then_inc(s_done, 1)
                    for _ in range(3):
                        next(v_steps)

            def attend(p, back):
                def transpose_p(n):
                    b, c = n // 4, n % 4
                    pe.wait_ge(norm_done, p.count(8, n + 1))
                    if n < 4:
                        pe.wait_ge(s_kept, p.count(8, 7 + n // 2))
                    else:
                        pe.wait_ge(pt_kept, p.count(8, n - 3))
                    for j in range(HC):
                        last = nc.tensor.transpose(att[:, n % 4, P * j:P * j + P], S[b][:, HC * c + j, 0:P], ident[:])
                    last.then_inc(pt_done, 1)

                transpose_p(0)
                transpose_p(1)
                transpose_p(2)
                if not back:
                    pe.wait_ge(klo_done, p.at(1).count(1, 1))
                for n in range(8):
                    if n + 3 < 8:
                        transpose_p(n + 3)
                    b, c = n // 4, n % 4
                    if back and c == 0:
                        pe.wait_ge(dn_done, p.at(-1).count(2, b + 1))
                    pe.wait_ge(pt_kept, p.count(8, n + 1))
                    for j in range(HC):
                        h = HC * c + j
                        last = nc.tensor.matmul(A[HD * j:HD * j + HD, b, P * c:P * c + P],
                                                v[:, b, HD * h:HD * h + HD], pT[:, n % 4, j, :],
                                                start=True, stop=True)
                    last.then_inc(av_done, 1)

            def project_out(q, b):
                pe.wait_ge(alo_done, q.count(2, b + 1))
                last = three_products(B[:, b, :], [((aT_hi[:, b, n, :], aT_lo[:, b, n, :]),
                                                    (wp_hi[:, n, :], wp_lo[:, n, :])) for n in range(NC)])
                last.then_inc(proj_done, 1)

            def modulated(q):
                pe.wait_ge(ylo_done, q.count(2, 2))
                for d in range(NC):
                    last = three_products(columns(A, d), [
                        ((l_hi[:, c, d, :], l_lo[:, c, d, :]),
                         (yx_hi[:, c].rearrange("p b l -> p (b l)"), yx_lo[:, c].rearrange("p b l -> p (b l)")))
                        for c in range(NC)])
                    if d % 2:
                        last.then_inc(l1_done, 1)

            def transposes(u, blocks):
                for n, block_ap in enumerate(blocks):
                    last = nc.tensor.transpose(bank(u)[:, P * n:P * n + P], block_ap, ident[:])
                last.then_inc(unit_done, 1)

            def image(u):
                for o in range(NC):
                    for n in range(NC):
                        last = nc.tensor.matmul(bank(u)[:, P * o:P * o + P], uT[n][:, P * o:P * o + P],
                                                condT[:, n, :], start=(n == 0), stop=(n == NC - 1))
                last.then_inc(unit_done, 1)

            pe.wait_ge(ident_ready, 2)
            pe.wait_ge(cond_loaded, 16)
            transposes(COND, [cond_nat[:, P * c:P * c + P] for c in range(NC)])
            by_chunk = cond_nat.rearrange("p (s c) -> p c s", c=NC)
            transposes(Y, [by_chunk[:, c, :] for c in range(NC)])
            pe.wait_ge(uk_loaded, 16)
            for n in range(NC):
                if n >= 2:
                    pe.wait_ge(unit_kept, n - 1)
                transposes(UK + n, [uk_nat[:, o, P * n:P * n + P] for o in range(NC)])
            transpose_x(Pair(0, 0), 0)
            pe.wait_ge(unit_kept, UK + NC)
            image(KIMG)
            pe.wait_ge(w_lo_done, NC)
            project_k(Pair(0, 0))
            project_q(Pair(0, 0), 0)
            pe.wait_ge(uv_loaded, 16)
            pe.wait_ge(unit_kept, KIMG + 1)
            for n in range(NC):
                transposes(UV + n, [uv_nat[:, o, P * n:P * n + P] for o in range(NC)])
            pe.wait_ge(unit_kept, UV + NC)
            image(VIMG)
            for n in range(NC):
                last = nc.tensor.matmul(bank(VROW), condT[:, n, :], uT[n], start=(n == 0), stop=(n == NC - 1))
            last.then_inc(unit_done, 1)
            pe.wait_ge(l_loaded, 16)
            l_by_chunk = l_nat.rearrange("p d (s c) -> p c d s", c=NC)
            for c in range(NC):
                if c == 2:
                    pe.wait_ge(unit_kept, VIMG + 1)
                if c == 3:
                    pe.wait_ge(vrow_ready, 2)
                transposes(L1 + c, [l_by_chunk[:, c, d, :] for d in range(NC)])
            pe.wait_ge(unit_kept, L1 + NC - 1)
            pe.wait_ge(l_lo_done, 1)
            for d in range(NC):
                for c in range(NC):
                    last = nc.tensor.matmul(bank(DN)[:, P * d:P * d + P], w_sq[:, c, d, :], ysq[:, c, :],
                                            start=(c == 0), stop=(c == NC - 1))
            last.then_inc(unit_done, 1)
            pe.wait_ge(l_lo_done, NC)
            pe.wait_ge(dn_step, 1)

            def step(p, back, ahead):
                scores_and_v(p, back)
                if ahead:
                    transpose_x(p.at(1), back)
                if back:
                    pe.wait_ge(v_kept, p.count(2, 1))
                    if back == 1:
                        pe.wait_ge(w_lo_done, NC + 1)
                    project_out(p.at(-1), 0)
                if ahead:
                    project_k(p.at(1))
                if back:
                    pe.wait_ge(v_kept, p.count(2, 2))
                    project_out(p.at(-1), 1)
                if ahead:
                    if not back:
                        pe.wait_ge(v_kept, p.count(2, 2))
                    project_q(p.at(1), back)
                if back:
                    if ahead:
                        pe.wait_ge(klo_done, p.at(1).count(1, 1))
                    modulated(p.at(-1))
                attend(p, back)

            run_pairs(pe, step)
            project_out(LAST, 0)
            project_out(LAST, 1)
            modulated(LAST)


_INS = ['x', 'cond_1024', 'mask_Bx1x1xS_ff0', 'L0_cond_c_attn_w', 'L0_cond_c_attn_b', 'L0_cond_c_proj_w',
        'L0_cond_c_proj_b', 'L0_cond_uk_w', 'L0_cond_uk_b', 'L0_cond_uv_w', 'L0_cond_uv_b', 'L1_cond_weight']


def kernel(**inputs):
    import numpy as _np
    import concourse.bacc as _bacc
    from concourse import mybir as _mybir
    from concourse.bass_utils import run_bass_kernel_spmd as _run

    nc = _bacc.Bacc("TRN2", target_bir_lowering=False, num_devices=1, dynamic_dma_scratch_size=1024)
    arrays, args = {}, []
    for name in _INS:
        a = _np.ascontiguousarray(inputs[name])
        arrays[f"in_{name}"] = a
        args.append(nc.dram_tensor(f"in_{name}", a.shape, _mybir.dt.from_np(a.dtype), kind="ExternalInput").ap())
    args.append(nc.dram_tensor("out_0", (NB, P, E), _mybir.dt.float32, kind="ExternalOutput").ap())
    build(nc, *args)
    r = _run(nc, [arrays], core_ids=[0])
    return r.results[0]["out_0"]
```

```python
from contextlib import ExitStack

import concourse.bass as bass
from concourse import mybir

ALU = mybir.AluOpType
ACT = mybir.ActivationFunctionType
F32 = mybir.dt.float32
F32R = mybir.dt.float32r

P = 128
NB = 128
PAIRS = NB // 2
UNROLL = 4
E = 512
NC = E // P
HD = 32
HC = P // HD
H = E // HD
KEYS = P + 1
IMG = P

KPAD = KEYS + 1
MASK_OUT = -10000.0
LOWEST = -3.4e38
QSCALE = float(HD) ** -0.5
WSCALE = float(E) ** -0.5
EPS = 1e-8


class Pair:

    def __init__(self, t, k):
        self.t, self.k = t, k

    def at(self, d):
        return Pair(self.t, self.k + d)

    @property
    def slot(self):
        return self.k % 2

    def count(self, per, n):
        return self.t * (UNROLL * per) + (self.k * per + n)

    def dma(self, n=1):
        return self.t * (UNROLL // 2 * 16) + (self.k // 2 + n) * 16

    def batch(self):
        return self.t * (2 * UNROLL) + self.k * 2


def build(nc, x, cond, mask, wqkv, bqkv, wproj, bproj, uk_w, uk_b, uv_w, uv_b, l1w, out):
    x_v = x.rearrange("b s e -> s b e")
    out_v = out.rearrange("b s e -> s b e")
    vrow_dram = nc.dram_tensor("v_rows", [NB, E], F32, kind="Internal").ap()

    with ExitStack() as ctx:
        def sb(name, shape, dt=F32):
            return ctx.enter_context(nc.sbuf_tensor(name, shape, dt))

        def sem(name):
            return ctx.enter_context(nc.semaphore(name))

        w_hi = sb("w_hi", [P, NC, 3 * E], F32R)
        w_lo = sb("w_lo", [P, NC, 3 * E], F32R)
        wp_hi = sb("wp_hi", [P, NC, E], F32R)
        wp_lo = sb("wp_lo", [P, NC, E], F32R)
        l_hi = sb("l_hi", [P, NC, NC, P], F32R)
        l_lo = sb("l_lo", [P, NC, NC, P], F32R)
        ident0 = sb("ident0", [P, P])
        ident = sb("ident", [P, P])
        qbias = sb("qbias", [P, NC])
        kbias = sb("kbias", [P, NC])
        ukbias = sb("ukbias", [P, NC])
        uvbias = sb("uvbias", [P, NC])
        pbias = sb("pbias", [P, E])
        kimgT = sb("kimgT", [P, NB, NC])
        vimgT = sb("vimgT", [P, NB, NC])
        ysc = sb("ysc", [P, NB, NC])
        dnorm = sb("dnorm", [P, NB, NC])
        vrow = sb("vrow", [P, 2, E])
        xin = sb("xin", [P, 2, 2, E])
        xb = sb("xb", [P, 2, 2, E])
        xT_hi = sb("xT_hi", [P, NC, 2, P], F32R)
        xT_lo = sb("xT_lo", [P, NC, 2, P], F32R)
        kc = sb("kc", [P, 2, NC, 2, KPAD])
        q_st = sb("q_st", [P, 2, NC, 2, P], F32R)
        k_hi = sb("k_hi", [P, 2, 2, NC, 2, KPAD], F32R)
        k_lo = sb("k_lo", [P, 2, 2, NC, 2, KPAD], F32R)
        cond_st = sb("cond_st", [P, 2, E])
        v = sb("v", [P, 2, E])
        S = [sb(f"S{b}", [P, H, KEYS]) for b in range(2)]
        pT = sb("pT", [P, 4, HC, P])
        aT_hi = sb("aT_hi", [P, 2, NC, P], F32R)
        aT_lo = sb("aT_lo", [P, 2, NC, P], F32R)
        yx = sb("yx", [P, NC, 2, P])
        yx_hi = sb("yx_hi", [P, NC, 2, P], F32R)
        yx_lo = sb("yx_lo", [P, NC, 2, P], F32R)
        maskb = sb("maskb", [P, 2, 2, KEYS])
        nmax = sb("nmax", [P, 2, H])
        pmax = sb("pmax", [P, 2, H])
        zsum = sb("zsum", [P, 2, H])
        rz = sb("rz", [P, 2, H])

        kc_hi, kc_lo = kc[:, 0], kc[:, 1]
        qc_hi, qc_lo = (t[:].rearrange("p b c q -> p (b c q)").rearrange("p (c q) -> p c q", c=NC)
                        for t in (aT_hi, aT_lo))

        att = ctx.enter_context(nc.psum_tensor("att", [P, 4, 512], F32))
        A = ctx.enter_context(nc.psum_tensor("A", [P, 2, 512], F32))
        B = ctx.enter_context(nc.psum_tensor("B", [P, 2, 512], F32))

        def rows_of(ap):
            return ap.rearrange("p (o i) -> p o i", o=NC)

        flat_S = [s[:].rearrange("p h k -> p (h k)") for s in S]
        flat_xb = xb[:].rearrange("p a b e -> p (a b e)")
        stages = flat_S[0], flat_S[1], flat_xb, pT[:].rearrange("p n h q -> p (n h q)")
        w_stage = [ap[:, 0:3 * E] for ap in stages]
        uk_nat = rows_of(kc[:].rearrange("p n c b k -> p (n c b k)")[:, 0:NC * E])
        uv_nat = [ap[:, 3 * E:4 * E] for ap in stages]
        wp_stage = flat_xb
        l_nat = [flat_S[d // 3][:, E * (d % 3):E * (d % 3) + E] for d in range(NC)]
        w_sq = pT
        uT = [v[:, 0, :], v[:, 1, :], xin[:, 1, 0, :], xin[:, 1, 1, :]]
        cond_nat, condT = cond_st[:, 0], cond_st[:, 1].rearrange("p (c b) -> p c b", c=NC)
        yx_flat = yx[:].rearrange("p c b t -> p (c b t)")
        uvb_bc, ysq = yx_flat[:, 0:E], yx_flat[:, E:2 * E].rearrange("p (c b) -> p c b", c=NC)
        vb_bc, vrow_st = vrow[:, 1, :], vrow[:, 0, :]
        dn_u, dn_r, dn_t = (ap.rearrange("p (d b) -> p d b", d=NC) for ap in (uvb_bc, cond_st[:, 0], cond_st[:, 1]))

        w_loaded = [sem(f"w_loaded{n}") for n in range(NC)]
        cond_loaded, uk_loaded, uv_loaded = sem("cond_loaded"), sem("uk_loaded"), sem("uv_loaded")
        l_loaded, wp_loaded, bias_loaded = sem("l_loaded"), sem("wp_loaded"), sem("bias_loaded")
        ident_ready, mask_zero, k_zero = sem("ident_ready"), sem("mask_zero"), sem("k_zero")
        w_hi_done, w_lo_done = sem("w_hi_done"), sem("w_lo_done")
        unit_done = sem("unit_done")
        unit_kept = sem("unit_kept")
        l_lo_done = sem("l_lo_done")
        vrow_ready, vrow_stored = sem("vrow_ready"), sem("vrow_stored")
        dn_step, dn_root = sem("dn_step"), sem("dn_root")

        x_loaded = [sem(f"x_loaded{n}") for n in range(2)]
        mask_loaded = [sem(f"mask_loaded{n}") for n in range(2)]
        stored = [sem(f"stored{n}") for n in range(2)]
        vrow_loaded = sem("vrow_loaded")
        xt_done = sem("xt_done")
        xhi_done = sem("xhi_done")
        xlo_done = sem("xlo_done")
        k_done, q_done, v_done = sem("k_done"), sem("q_done"), sem("v_done")
        khi_done, qhi_done, v_kept = sem("khi_done"), sem("qhi_done"), sem("v_kept")
        s_done, s_kept = sem("s_done"), sem("s_kept")
        sel_done = sem("sel_done")
        klo_done, qlo_done = sem("klo_done"), sem("qlo_done")
        k_placed, q_placed = sem("k_placed"), sem("q_placed")
        k_copied = sem("k_copied")
        sel_seen, s_seen = sem("sel_seen"), sem("s_seen")
        rowmax_done, max_done = sem("rowmax_done"), sem("max_done")
        exp_done = sem("exp_done")
        rz_done = sem("rz_done")
        norm_done = sem("norm_done")
        pt_done, pt_kept = sem("pt_done"), sem("pt_kept")
        av_done = sem("av_done")
        ahi_done, alo_done = sem("ahi_done"), sem("alo_done")
        proj_done = sem("proj_done")
        xb_done = sem("xb_done")
        x1_done = sem("x1_done")
        yx_done = sem("yx_done")
        yhi_done, ylo_done = sem("yhi_done"), sem("ylo_done")
        l1_done = sem("l1_done")
        out_done = sem("out_done")

        block = ctx.enter_context(nc.Block())

        def columns(unit, c):
            return unit[:, c // 2, 256 * (c % 2):256 * (c % 2) + 256]

        def run_pairs(eng, step):
            step(Pair(0, 0), 0, 2)
            step(Pair(0, 1), 1, 2)
            with eng.Fori(0, (PAIRS - 4) // UNROLL) as t:
                for k in range(2, 2 + UNROLL):
                    step(Pair(t, k), 2, 2)
            step(Pair(0, PAIRS - 2), 2, 1)
            step(Pair(0, PAIRS - 1), 2, 0)

        LAST = Pair(0, PAIRS - 1)

        COND, Y, UK, KIMG, UV, VIMG, VROW, L1, DN = 0, 1, 2, 6, 7, 11, 12, 13, 17

        def bank(u):
            return att[:, u % 4, :]

        def chunked(u):
            return bank(u).rearrange("p (c n) -> p c n", c=NC)

        @block.sync
        def _(sp):
            def load_x(p):
                sp.dma_start(xin[:, p.slot], x_v[:, bass.ds(p.batch(), 2), :]).then_inc(x_loaded[p.slot], 16)

            def load_mask(p):
                rows = mask[bass.ds(p.batch(), 2), 0, 0, :].partition_broadcast(P)
                sp.dma_start(maskb[:, p.slot, :, 0:P], rows).then_inc(mask_loaded[p.slot], 16)

            def place_k(p):
                for done, src, dst in ((khi_done, kc_hi, k_hi), (klo_done, kc_lo, k_lo)):
                    sp.wait_ge(done, p.count(1, 1))
                    flat = src.rearrange("p c b k -> p (c b k)")
                    for s in range(2):
                        for a in range(2):
                            src_row, row = 64 * s + HD * a, 64 * (1 - s) + HD * a
                            to = dst[row:row + HD, s, a].bitcast(F32).rearrange("p c b k -> p (c b k)")
                            sp.dma_start(to, flat[src_row:src_row + HD]).then_inc(k_placed, 16)

            def place_q(p):
                for part, (done, src) in enumerate(((qhi_done, qc_hi), (qlo_done, qc_lo))):
                    sp.wait_ge(done, p.count(2, 2))
                    for s in range(2):
                        to = q_st[64 * part:64 * part + 64, s].bitcast(F32).rearrange("p c b q -> p (c b q)")
                        sp.dma_start(to, src[64 * s:64 * s + 64].bitcast(F32).rearrange("p c q -> p (c q)"))\
                            .then_inc(q_placed, 16)

            def load_vrow(p):
                rows = vrow_dram[bass.ds(p.batch(), 2), :].partition_broadcast(P)
                sp.dma_start(vrow[:], rows).then_inc(vrow_loaded, 16)

            w_v = wqkv.rearrange("(c p) n -> p c n", p=P)
            sp.dma_start(cond_nat, cond).then_inc(cond_loaded, 16)
            load_x(Pair(0, 0))
            sp.dma_start(uk_nat, uk_w.rearrange("(o p) i -> p o i", p=P)).then_inc(uk_loaded, 16)
            for c in range(NC):
                sp.dma_start(w_stage[c], w_v[:, c, :]).then_inc(w_loaded[c], 16)
                if c == 0:
                    for dst, src in ((qbias, bqkv[0:E]), (kbias, bqkv[E:2 * E]), (ukbias, uk_b), (uvbias, uv_b)):
                        sp.dma_start(dst[:], src.rearrange("(c p) -> p c", p=P),
                                     allow_slow_non_contiguous=True).then_inc(bias_loaded, 16)
                    for dst, src in ((pbias[:], bproj), (vb_bc, bqkv[2 * E:3 * E]), (uvb_bc, uv_b)):
                        sp.dma_start(dst, src.partition_broadcast(P)).then_inc(bias_loaded, 16)
            for o in range(NC):
                sp.dma_start(uv_nat[o], uv_w[P * o:P * o + P, :]).then_inc(uv_loaded, 16)
            sp.wait_ge(w_hi_done, 2)
            sp.wait_ge(w_lo_done, 2)
            l_v = l1w[0, :, :, 0].rearrange("(s d) i -> d s i", d=NC)
            for d in range(NC):
                sp.dma_start(l_nat[d], l_v[d]).then_inc(l_loaded, 16)
            sp.wait_ge(w_hi_done, 3)
            sp.wait_ge(w_lo_done, 3)
            sp.wait_ge(unit_done, UV + NC)
            sp.dma_start(rows_of(wp_stage), wproj.rearrange("(c p) n -> p c n", p=P)).then_inc(wp_loaded, 16)
            sp.wait_ge(mask_zero, 1)
            load_mask(Pair(0, 0))
            sp.wait_ge(k_zero, 3)
            place_k(Pair(0, 0))
            place_q(Pair(0, 0))
            sp.wait_ge(vrow_ready, 2)
            sp.dma_start(vrow_dram, vrow_st).then_inc(vrow_stored, 16)
            sp.wait_ge(unit_done, VROW + 1)
            load_x(Pair(0, 1))
            sp.wait_ge(vrow_stored, 16)
            load_vrow(Pair(0, 0))

            def store(q):
                sp.wait_ge(out_done, q.count(2, 2))
                sp.dma_start(out_v[:, bass.ds(q.batch(), 2), :], xb[:, q.slot]).then_inc(stored[q.slot], 16)

            def step(p, back, ahead):
                if ahead:
                    if back:
                        sp.wait_ge(max_done, p.at(-1).count(2, 2))
                    load_mask(p.at(1))
                    sp.wait_ge(v_kept, p.count(2, 2))
                    load_vrow(p.at(1))
                    place_k(p.at(1))
                    place_q(p.at(1))
                if ahead > 1:
                    sp.wait_ge(xb_done, p.count(1, 1))
                    load_x(p.at(2))
                if back:
                    store(p.at(-1))

            run_pairs(sp, step)
            store(LAST)
            for n in range(2):
                sp.wait_ge(stored[n], 16 * (PAIRS // 2))

        @block.gpsimd
        def _(pool):
            nc.gpsimd.memset(ident0[:], 0.0).then_inc(ident_ready, 1)
            pool.wait_ge(ident_ready, 1)
            nc.gpsimd.affine_select(out=ident[:], in_=ident0[:], compare_op=ALU.not_equal, fill=1.0, base=0,
                                    pattern=[[-1, P]], channel_multiplier=1).then_inc(ident_ready, 1)
            nc.gpsimd.memset(maskb[:, :, :, IMG:KEYS], 0.0).then_inc(mask_zero, 1)
            nc.gpsimd.memset(k_hi[:].bitcast(F32), 0.0).then_inc(k_zero, 1)
            nc.gpsimd.memset(k_lo[:].bitcast(F32), 0.0).then_inc(k_zero, 1)
            pool.wait_ge(unit_done, UK + NC)
            nc.gpsimd.memset(kc[:, :, :, :, KEYS:KPAD], 0.0).then_inc(k_zero, 1)

            mask_out = pool.to_reg(MASK_OUT)

            def scale_y(q, b):
                pool.wait_ge(x1_done, q.count(2, b + 1))
                nc.gpsimd.tensor_tensor(
                    yx[:, :, b, :], xb[:, q.slot, b].rearrange("p (c l) -> p c l", c=NC),
                    ysc[:, q.batch() + b, :].unsqueeze(2).to_broadcast([P, NC, P]),
                    ALU.mult).then_inc(yx_done, 1)

            def normalize(p, b):
                pool.wait_ge(rz_done, p.count(2, b + 1))
                for c in range(NC):
                    heads = slice(HC * c, HC * c + HC)
                    s = S[b][:, heads, 0:P]
                    nc.gpsimd.tensor_tensor(s, s, rz[:, b, heads].unsqueeze(2).to_broadcast([P, HC, P]),
                                            ALU.mult).then_inc(norm_done, 1)

            def add_bias(p, back):
                pool.wait_ge(x_loaded[p.slot], p.dma())
                if back == 0:
                    pool.wait_ge(bias_loaded, 16 * 7)
                    pool.wait_ge(w_hi_done, NC + 1)
                    pool.wait_ge(w_lo_done, NC + 1)
                if back == 2:
                    pool.wait_ge(stored[p.slot], p.at(-2).dma())
                nc.gpsimd.tensor_tensor(xb[:, p.slot], xin[:, p.slot],
                                        pbias[:].unsqueeze(1).to_broadcast([P, 2, E]), ALU.add).then_inc(xb_done, 1)

            def step(p, back, ahead):
                for b in range(2):
                    for g in range(2):
                        pool.wait_ge(s_kept, p.count(8, 4 * b + 2 * g + 2))
                        pool.sem_inc(s_seen, 1)
                        s = S[b][:, 8 * g:8 * g + 8, 0:P]
                        nc.gpsimd.affine_select(out=s, in_=s, compare_op=ALU.is_ge, fill=mask_out, base=0,
                                                pattern=[[0, 8], [-1, P]], channel_multiplier=1)\
                            .then_inc(sel_done, 1)
                add_bias(p, back)
                if back:
                    scale_y(p.at(-1), 0)
                if ahead:
                    normalize(p, 0)
                if back:
                    scale_y(p.at(-1), 1)
                if not ahead:
                    normalize(p, 0)
                normalize(p, 1)

            run_pairs(pool, step)
            scale_y(LAST, 0)
            scale_y(LAST, 1)

        @block.scalar
        def _(act):
            def keep_xT_hi(p):
                act.wait_ge(xt_done, p.count(2, 2))
                nc.scalar.activation(xT_hi[:].rearrange("p e b t -> p b e t"),
                                     A[:].rearrange("p b (e t) -> p b e t", e=NC), ACT.Copy).then_inc(xhi_done, 1)

            def keep_q_hi(p):
                for c in range(NC):
                    if c % 2 == 0:
                        act.wait_ge(q_done, p.count(2, c // 2 + 1))
                    last = nc.scalar.activation(qc_hi[:, c, :], columns(B, c), ACT.Identity, bias=qbias[:, c:c + 1])
                    if c % 2:
                        last.then_inc(qhi_done, 1)

            def keep_k_hi(p):
                act.wait_ge(k_done, p.count(1, 1))
                for c in range(NC):
                    nc.scalar.activation(kc_hi[:, c, :, 0:P].bitcast(F32R),
                                         columns(A, c).rearrange("p (b t) -> p b t", b=2), ACT.Identity,
                                         bias=kbias[:, c:c + 1])
                nc.scalar.activation(kc_hi[:, :, :, IMG].bitcast(F32R).rearrange("p c b -> p b c"),
                                     kimgT[:, bass.ds(p.batch(), 2), :], ACT.Copy).then_inc(khi_done, 1)

            def exps(p, b, heads):
                if heads[0] == 0:
                    act.wait_ge(max_done, p.count(2, b + 1))
                for h in heads:
                    last = nc.scalar.activation(S[b][:, h, :], S[b][:, h, :], ACT.Exp, bias=nmax[:, b, h:h + 1],
                                                accum_out=zsum[:, b, h:h + 1])
                if h == H - 1:
                    last.then_inc(exp_done, 1)

            def keep_yx_hi(q, b):
                act.wait_ge(yx_done, q.count(2, b + 1))
                nc.scalar.activation(yx_hi[:, :, b], yx[:, :, b], ACT.Copy).then_inc(yhi_done, 1)

            def keep_unit(u, out_ap, in_ap):
                act.wait_ge(unit_done, u + 1)
                return nc.scalar.activation(out_ap, in_ap, ACT.Copy)

            def keep_image(u, dst, bias):
                act.wait_ge(unit_done, u + 1)
                for c in range(NC):
                    last = nc.scalar.activation(dst[:, :, c], bank(u)[:, P * c:P * c + P], ACT.Identity,
                                                bias=bias[:, c:c + 1])
                last.then_inc(unit_kept, 1)

            def keep_w_hi(c):
                act.wait_ge(w_loaded[c], 16)
                nc.scalar.activation(w_hi[:, c, :], w_stage[c], ACT.Copy).then_inc(w_hi_done, 1)

            keep_unit(COND, condT, chunked(COND)).then_inc(unit_kept, 1)
            keep_unit(Y, ysc[:].rearrange("p b c -> p c b"), chunked(Y))
            nc.scalar.activation(ysq, chunked(Y), ACT.Square).then_inc(unit_kept, 1)
            keep_xT_hi(Pair(0, 0))
            for n in range(NC):
                keep_unit(UK + n, uT[n], bank(UK + n)).then_inc(unit_kept, 1)
            keep_w_hi(0)
            keep_w_hi(1)
            act.wait_ge(bias_loaded, 16 * 7)
            keep_image(KIMG, kimgT, ukbias)
            keep_w_hi(2)
            keep_w_hi(3)
            act.wait_ge(unit_kept, KIMG + 1)
            keep_k_hi(Pair(0, 0))
            for n in range(NC):
                keep_unit(UV + n, uT[n], bank(UV + n)).then_inc(unit_kept, 1)
            keep_q_hi(Pair(0, 0))
            keep_image(VIMG, vimgT, uvbias)
            act.wait_ge(w_lo_done, NC)
            for c in range(NC):
                keep_unit(L1 + c, l_hi[:, c].rearrange("p d s -> p (d s)"), bank(L1 + c))
                nc.scalar.activation(w_sq[:, c].rearrange("p d s -> p (d s)"), bank(L1 + c),
                                     ACT.Square).then_inc(unit_kept, 1)
            act.wait_ge(wp_loaded, 16)
            nc.scalar.activation(wp_hi[:].rearrange("p c n -> p (c n)"), wp_stage, ACT.Copy).then_inc(w_hi_done, 1)

            def step(p, back, ahead):
                for n in range(8):
                    act.wait_ge(s_done, p.count(8, n + 1))
                    c = n % 4
                    scores = att[:, 2 * (n % 2):2 * (n % 2) + 2, 0:2 * KPAD].rearrange("p s (a k) -> p s a k", a=2)
                    nc.scalar.activation(S[n // 4][:, HC * c:HC * c + HC, :].rearrange("p (s a) k -> p s a k", a=2),
                                         scores[:, :, :, 0:KEYS], ACT.Copy, scale=QSCALE).then_inc(s_kept, 1)
                    if n == 0 and back:
                        keep_aT_hi(p.at(-1), 1)
                if ahead:
                    keep_xT_hi(p.at(1))
                exps(p, 0, range(H))
                exps(p, 1, range(0, 4))
                if ahead:
                    keep_k_hi(p.at(1))
                if back:
                    keep_yx_hi(p.at(-1), 0)
                exps(p, 1, range(4, 10 if ahead else 6))
                if back:
                    keep_yx_hi(p.at(-1), 1)
                exps(p, 1, range(10 if ahead else 6, H))
                if ahead:
                    keep_q_hi(p.at(1))
                for n in range(8):
                    act.wait_ge(pt_done, p.count(8, n + 1))
                    if n >= 4 or back:
                        act.wait_ge(av_done, p.count(8, n - 3))
                    nc.scalar.activation(pT[:, n % 4].rearrange("p h q -> p (h q)"), att[:, n % 4, :],
                                         ACT.Copy).then_inc(pt_kept, 1)
                    if n == 5 and not ahead:
                        keep_aT_hi(p, 0)
                if ahead:
                    act.wait_ge(q_placed, p.at(1).count(64, 64))
                    keep_aT_hi(p, 0)
                if not back:
                    act.wait_ge(dn_step, 1)
                    nc.scalar.activation(dn_r, dn_u, ACT.Sqrt).then_inc(dn_root, 1)

            def keep_aT_hi(p, b):
                act.wait_ge(av_done, p.count(8, 4 * b + 4))
                for c in range(NC):
                    last = nc.scalar.activation(aT_hi[:, b, c, :], A[:, b, P * c:P * c + P], ACT.Identity,
                                                bias=vimgT[:, p.batch() + b, c:c + 1])
                last.then_inc(ahi_done, 1)

            run_pairs(act, step)
            keep_aT_hi(LAST, 1)
            keep_yx_hi(LAST, 0)
            keep_yx_hi(LAST, 1)

        @block.vector
        def _(dve):
            def splits_low(out_ap, in_ap, hi_ap):
                return nc.vector.tensor_tensor(out_ap, in_ap, hi_ap.bitcast(F32), ALU.subtract)

            def keep_xT_lo(p):
                dve.wait_ge(xhi_done, p.count(1, 1))
                splits_low(xT_lo[:].rearrange("p e b t -> p b e t"), A[:].rearrange("p b (e t) -> p b e t", e=NC),
                           xT_hi[:].rearrange("p e b t -> p b e t")).then_inc(xlo_done, 1)

            def keep_k_lo(p):
                dve.wait_ge(khi_done, p.count(1, 1))
                for c in range(NC):
                    nc.vector.scalar_tensor_tensor(
                        out=kc_lo[:, c, :, 0:P].bitcast(F32R), in0=columns(A, c).rearrange("p (b t) -> p b t", b=2),
                        scalar=kbias[:, c:c + 1], in1=kc_hi[:, c, :, 0:P], op0=ALU.add, op1=ALU.subtract)
                nc.vector.tensor_tensor(
                    kc_lo[:, :, :, IMG].bitcast(F32R).rearrange("p c b -> p b c"),
                    kimgT[:, bass.ds(p.batch(), 2), :], kc_hi[:, :, :, IMG].rearrange("p c b -> p b c"),
                    ALU.subtract).then_inc(klo_done, 1)

            def copy_k(src, dst):
                for s in range(2):
                    for a in range(2):
                        row = 64 * s + HD * a
                        last = nc.vector.tensor_copy(dst[row:row + HD, s, a].rearrange("p c b k -> p (c b k)"),
                                                     src[row:row + HD].rearrange("p c b k -> p (c b k)"))
                last.then_inc(k_copied, 1)

            def keep_q_lo(p):
                for c in range(NC):
                    if c % 2 == 0:
                        dve.wait_ge(qhi_done, p.count(2, c // 2 + 1))
                    last = nc.vector.scalar_tensor_tensor(
                        out=qc_lo[:, c, :], in0=columns(B, c), scalar=qbias[:, c:c + 1],
                        in1=qc_hi[:, c, :].bitcast(F32), op0=ALU.add, op1=ALU.subtract)
                    if c % 2:
                        last.then_inc(qlo_done, 1)

            def keep_v(p, b):
                dve.wait_ge(vrow_loaded, p.count(16, 16))
                dve.wait_ge(v_done, p.count(2, b + 1))
                nc.vector.tensor_tensor(v[:, b, :], B[:, b, :], vrow[:, b, :], ALU.add).then_inc(v_kept, 1)

            def row_max(p, b):
                if b == 0:
                    dve.wait_ge(mask_loaded[p.slot], p.dma())
                for h in range(H):
                    if h % 8 == 0:
                        dve.wait_ge(sel_done, p.count(4, 2 * b + h // 8 + 1))
                        dve.sem_inc(sel_seen, 1)
                    last = nc.vector.tensor_tensor_reduce(
                        out=S[b][:, h, :], in0=S[b][:, h, :], in1=maskb[:, p.slot, b, :], scale=1.0, scalar=LOWEST,
                        op0=ALU.add, op1=ALU.max, accum_out=pmax[:, b, h:h + 1])
                last.then_inc(rowmax_done, 1)
                dve.wait_ge(rowmax_done, p.count(2, b + 1))
                nc.vector.tensor_scalar(nmax[:, b, :], pmax[:, b, :], -1.0, None, ALU.mult).then_inc(max_done, 1)

            def invert_sum(p, b):
                dve.wait_ge(exp_done, p.count(2, b + 1))
                nc.vector.reciprocal(rz[:, b, :], zsum[:, b, :]).then_inc(rz_done, 1)

            def first_residual(q, b):
                if b == 0:
                    dve.wait_ge(xb_done, q.count(1, 1))
                dve.wait_ge(proj_done, q.count(2, b + 1))
                nc.vector.tensor_tensor(xb[:, q.slot, b], B[:, b, :], xb[:, q.slot, b], ALU.add).then_inc(x1_done, 1)

            def keep_yx_lo(q, b):
                dve.wait_ge(yhi_done, q.count(2, b + 1))
                splits_low(yx_lo[:, :, b], yx[:, :, b], yx_hi[:, :, b]).then_inc(ylo_done, 1)

            def demodulate(q, unit):
                for a in range(2):
                    dve.wait_ge(l1_done, q.count(2, a + 1))
                    for d in range(2 * a, 2 * a + 2):
                        for b in range(2):
                            x1 = xb[:, q.slot, b, P * d:P * d + P]
                            last = nc.vector.scalar_tensor_tensor(
                                out=x1, in0=columns(unit, d)[:, P * b:P * b + P],
                                scalar=dnorm[:, q.batch() + b, d:d + 1], in1=x1, op0=ALU.mult, op1=ALU.add)
                    last.then_inc(out_done, 1)

            def keep_aT_lo(p, b):
                dve.wait_ge(ahi_done, p.count(2, b + 1))
                for c in range(NC):
                    last = nc.vector.scalar_tensor_tensor(
                        out=aT_lo[:, b, c, :], in0=A[:, b, P * c:P * c + P],
                        scalar=vimgT[:, p.batch() + b, c:c + 1], in1=aT_hi[:, b, c, :].bitcast(F32),
                        op0=ALU.add, op1=ALU.subtract)
                last.then_inc(alo_done, 1)

            keep_xT_lo(Pair(0, 0))
            for c in range(NC):
                dve.wait_ge(w_hi_done, c + 1)
                splits_low(w_lo[:, c, :], w_stage[c], w_hi[:, c, :]).then_inc(w_lo_done, 1)
            dve.wait_ge(bias_loaded, 16 * 7)
            nc.vector.tensor_tensor(vb_bc, vb_bc, uvb_bc, ALU.subtract).then_inc(vrow_ready, 1)
            keep_k_lo(Pair(0, 0))
            dve.wait_ge(k_zero, 3)
            copy_k(kc_hi, k_hi)
            keep_q_lo(Pair(0, 0))
            dve.wait_ge(klo_done, 1)
            copy_k(kc_lo, k_lo)
            dve.wait_ge(unit_done, VROW + 1)
            dve.wait_ge(vrow_ready, 1)
            nc.vector.tensor_tensor(vrow_st, vb_bc, bank(VROW), ALU.subtract).then_inc(vrow_ready, 1)
            for c in range(NC):
                dve.wait_ge(unit_kept, L1 + c)
                splits_low(l_lo[:, c].rearrange("p d s -> p (d s)"), bank(L1 + c),
                           l_hi[:, c].rearrange("p d s -> p (d s)")).then_inc(l_lo_done, 1)
            dve.wait_ge(w_hi_done, NC + 1)
            splits_low(wp_lo[:].rearrange("p c n -> p (c n)"), wp_stage,
                       wp_hi[:].rearrange("p c n -> p (c n)")).then_inc(w_lo_done, 1)

            def take_demod_sum():
                dve.wait_ge(unit_done, DN + 1)
                nc.vector.tensor_scalar(dn_u, chunked(DN), WSCALE * WSCALE, EPS, ALU.mult, ALU.add)\
                    .then_inc(dn_step, 1)

            def invert_demod_root():
                dve.wait_ge(dn_root, 1)
                nc.vector.reciprocal(dn_t, dn_r).then_inc(dn_step, 1)
                dve.wait_ge(dn_step, 2)
                nc.vector.tensor_tensor(dn_r, dn_t, dn_t, ALU.mult).then_inc(dn_step, 1)
                dve.wait_ge(dn_step, 3)
                nc.vector.tensor_tensor(dn_r, dn_r, dn_u, ALU.mult).then_inc(dn_step, 1)
                dve.wait_ge(dn_step, 4)
                nc.vector.tensor_scalar(dn_r, dn_r, -0.5, 1.5, ALU.mult, ALU.add).then_inc(dn_step, 1)
                dve.wait_ge(dn_step, 5)
                nc.vector.scalar_tensor_tensor(out=dnorm[:].rearrange("p b d -> p d b"), in0=dn_t, scalar=WSCALE,
                                               in1=dn_r, op0=ALU.mult, op1=ALU.mult).then_inc(dn_step, 1)
                dve.wait_ge(dn_step, 6)

            def step(p, back, ahead):
                keep_v(p, 0)
                row_max(p, 0)
                keep_v(p, 1)
                if ahead:
                    keep_xT_lo(p.at(1))
                row_max(p, 1)
                if not back:
                    take_demod_sum()
                if back:
                    first_residual(p.at(-1), 0)
                invert_sum(p, 0)
                if back:
                    first_residual(p.at(-1), 1)
                if ahead:
                    keep_k_lo(p.at(1))
                if back:
                    keep_yx_lo(p.at(-1), 0)
                    keep_yx_lo(p.at(-1), 1)
                if ahead:
                    copy_k(kc_hi, k_hi)
                invert_sum(p, 1)
                if ahead:
                    keep_q_lo(p.at(1))
                    dve.wait_ge(klo_done, p.at(1).count(1, 1))
                    copy_k(kc_lo, k_lo)
                if back:
                    demodulate(p.at(-1), A if ahead else B)
                keep_aT_lo(p, 0)
                if not back:
                    invert_demod_root()
                keep_aT_lo(p, 1)

            run_pairs(dve, step)
            first_residual(LAST, 0)
            first_residual(LAST, 1)
            keep_yx_lo(LAST, 0)
            keep_yx_lo(LAST, 1)
            demodulate(LAST, A)

        @block.tensor
        def _(pe):
            def transpose(out_ap, in_ap):
                return nc.tensor.transpose(out_ap, in_ap, ident[:])

            def three_products(out_ap, lhs_rhs_pairs):
                n = len(lhs_rhs_pairs)
                for i, ((l_h, l_l), (r_h, r_l)) in enumerate(lhs_rhs_pairs):
                    nc.tensor.matmul(out_ap, l_h, r_h, start=(i == 0), stop=False)
                    nc.tensor.matmul(out_ap, l_h, r_l, start=False, stop=False)
                    last = nc.tensor.matmul(out_ap, l_l, r_h, start=False, stop=(i == n - 1))
                return last

            def transpose_x(p, back):
                pe.wait_ge(x_loaded[p.slot], p.dma())
                if back:
                    pe.wait_ge(alo_done, p.at(-2).count(2, 2))
                for b in range(2):
                    for c in range(NC):
                        last = transpose(A[:, b, P * c:P * c + P], xin[:, p.slot, b, P * c:P * c + P])
                    last.then_inc(xt_done, 1)

            def x_moving(n):
                return xT_hi[:, n].rearrange("p b t -> p (b t)"), xT_lo[:, n].rearrange("p b t -> p (b t)")

            def project_k(p):
                pe.wait_ge(xlo_done, p.count(1, 1))
                for c in range(NC):
                    w = slice(E + P * c, E + P * c + P)
                    last = three_products(columns(A, c), [((w_hi[:, n, w], w_lo[:, n, w]), x_moving(n))
                                                          for n in range(NC)])
                last.then_inc(k_done, 1)

            def project_q(p, back):
                for c in range(NC):
                    if back and c % 2 == 0:
                        pe.wait_ge(x1_done, p.at(-2).count(2, c // 2 + 1))
                    w = slice(P * c, P * c + P)
                    last = three_products(columns(B, c), [((w_hi[:, n, w], w_lo[:, n, w]), x_moving(n))
                                                          for n in range(NC)])
                    if c % 2:
                        last.then_inc(q_done, 1)

            def project_v(p):
                for b in range(2):
                    pe.wait_ge(qlo_done, p.count(2, b + 1))
                    for n in range(NC):
                        x_h, x_l, w_h, w_l = xT_hi[:, n, b, :], xT_lo[:, n, b, :], w_hi[:, n, 2 * E:], w_lo[:, n, 2 * E:]
                        for m, (left, right) in enumerate(((x_h, w_h), (x_h, w_l), (x_l, w_h))):
                            last = nc.tensor.matmul(B[:, b, :], left, right, start=(n == m == 0),
                                                    stop=(n == NC - 1 and m == 2))
                            if n == NC - 1 and m == 2:
                                last.then_inc(v_done, 1)
                            yield

            def scores_and_v(p, back):
                v_steps = project_v(p)
                if not back:
                    for _ in range(3 * NC):
                        next(v_steps)
                    pe.wait_ge(unit_kept, L1 + NC - 1)
                    pe.wait_ge(l_lo_done, NC)
                pe.wait_ge(q_placed, p.count(64, 64))
                pe.wait_ge(k_placed, p.count(128, 128))
                pe.wait_ge(k_copied, p.count(2, 2))
                for n in range(8):
                    b, c = n // 4, n % 4
                    if n >= 2:
                        pe.wait_ge(s_kept, p.count(8, n - 1))
                    elif back:
                        pe.wait_ge(pt_kept, p.at(-1).count(8, 6 + 2 * n))
                    for s in range(2):
                        q = q_st[:, s, c, b, :]
                        to = att[:, 2 * (n % 2) + s, 0:2 * KPAD]
                        nc.tensor.matmul(to, q, k_hi[:, s, :, c, b, :], start=True, stop=False)
                        last = nc.tensor.matmul(to, q, k_lo[:, s, :, c, b, :], start=False, stop=True)
                    last.then_inc(s_done, 1)
                    for _ in range(3):
                        next(v_steps, None)

            def attend(p, back, ahead):
                def transpose_p(n):
                    b, c = n // 4, n % 4
                    pe.wait_ge(norm_done, p.count(8, n + 1))
                    if n < 4:
                        pe.wait_ge(s_kept, p.count(8, 7 + n // 2))
                    else:
                        pe.wait_ge(pt_kept, p.count(8, n - 3))
                    for j in range(HC):
                        last = transpose(att[:, n % 4, P * j:P * j + P], S[b][:, HC * c + j, 0:P])
                    last.then_inc(pt_done, 1)

                lead = 3 if ahead else 4
                for n in range(lead):
                    transpose_p(n)
                if not ahead:
                    modulated(p.at(-1), B)
                for n in range(8):
                    if n + lead < 8:
                        transpose_p(n + lead)
                    b, c = n // 4, n % 4
                    if back and ahead and c == 0:
                        pe.wait_ge(out_done, p.at(-1).count(2, b + 1))
                    pe.wait_ge(pt_kept, p.count(8, n + 1))
                    for j in range(HC):
                        h = HC * c + j
                        last = nc.tensor.matmul(A[HD * j:HD * j + HD, b, P * c:P * c + P],
                                                v[:, b, HD * h:HD * h + HD], pT[:, n % 4, j, :],
                                                start=True, stop=True)
                    last.then_inc(av_done, 1)

            def project_out(q, b):
                pe.wait_ge(alo_done, q.count(2, b + 1))
                last = three_products(B[:, b, :], [((aT_hi[:, b, n, :], aT_lo[:, b, n, :]),
                                                    (wp_hi[:, n, :], wp_lo[:, n, :])) for n in range(NC)])
                last.then_inc(proj_done, 1)

            def modulated(q, unit):
                pe.wait_ge(ylo_done, q.count(2, 2))
                for d in range(NC):
                    last = three_products(columns(unit, d), [
                        ((l_hi[:, c, d, :], l_lo[:, c, d, :]),
                         (yx_hi[:, c].rearrange("p b l -> p (b l)"), yx_lo[:, c].rearrange("p b l -> p (b l)")))
                        for c in range(NC)])
                    if d % 2:
                        last.then_inc(l1_done, 1)

            def transposes(u, blocks):
                for n, block_ap in enumerate(blocks):
                    last = transpose(bank(u)[:, P * n:P * n + P], block_ap)
                last.then_inc(unit_done, 1)

            def image(u):
                for o in range(NC):
                    for n in range(NC):
                        last = nc.tensor.matmul(bank(u)[:, P * o:P * o + P], uT[n][:, P * o:P * o + P],
                                                condT[:, n, :], start=(n == 0), stop=(n == NC - 1))
                last.then_inc(unit_done, 1)

            pe.wait_ge(ident_ready, 2)
            pe.wait_ge(cond_loaded, 16)
            transposes(COND, [cond_nat[:, P * c:P * c + P] for c in range(NC)])
            by_chunk = cond_nat.rearrange("p (s c) -> p c s", c=NC)
            transposes(Y, [by_chunk[:, c, :] for c in range(NC)])
            transpose_x(Pair(0, 0), 0)
            pe.wait_ge(uk_loaded, 16)
            for n in range(NC):
                if n >= 2:
                    pe.wait_ge(unit_kept, n - 1)
                transposes(UK + n, [uk_nat[:, o, P * n:P * n + P] for o in range(NC)])
            pe.wait_ge(unit_kept, UK + NC)
            image(KIMG)
            pe.wait_ge(w_lo_done, NC)
            project_k(Pair(0, 0))
            pe.wait_ge(uv_loaded, 16 * NC)
            pe.wait_ge(unit_kept, KIMG + 1)
            for n in range(NC):
                transposes(UV + n, [uv_nat[o][:, P * n:P * n + P] for o in range(NC)])
            project_q(Pair(0, 0), 0)
            pe.wait_ge(unit_kept, UV + NC)
            image(VIMG)
            for n in range(NC):
                last = nc.tensor.matmul(bank(VROW), condT[:, n, :], uT[n], start=(n == 0), stop=(n == NC - 1))
            last.then_inc(unit_done, 1)
            pe.wait_ge(l_loaded, 16 * NC)
            l_by_chunk = [rows.rearrange("p (s c) -> p c s", c=NC) for rows in l_nat]
            for c in range(NC):
                if c == 2:
                    pe.wait_ge(unit_kept, VIMG + 1)
                if c == 3:
                    pe.wait_ge(vrow_ready, 2)
                transposes(L1 + c, [l_by_chunk[d][:, c, :] for d in range(NC)])

            def demod_sums(p):
                pe.wait_ge(s_kept, p.count(8, 7))
                for d in range(NC):
                    for c in range(NC):
                        last = nc.tensor.matmul(bank(DN)[:, P * d:P * d + P], w_sq[:, c, d, :], ysq[:, c, :],
                                                start=(c == 0), stop=(c == NC - 1))
                last.then_inc(unit_done, 1)

            def step(p, back, ahead):
                scores_and_v(p, back)
                if ahead:
                    transpose_x(p.at(1), back)
                if not back:
                    demod_sums(p)
                if back:
                    pe.wait_ge(v_kept, p.count(2, 1))
                    if back == 1:
                        pe.wait_ge(w_lo_done, NC + 1)
                    project_out(p.at(-1), 0)
                if ahead:
                    project_k(p.at(1))
                if back:
                    pe.wait_ge(v_kept, p.count(2, 2))
                    project_out(p.at(-1), 1)
                if ahead:
                    if not back:
                        pe.wait_ge(v_kept, p.count(2, 2))
                    project_q(p.at(1), back)
                    pe.wait_ge(klo_done, p.at(1).count(1, 1))
                    if back:
                        modulated(p.at(-1), A)
                    else:
                        pe.wait_ge(dn_step, 1)
                attend(p, back, ahead)

            run_pairs(pe, step)
            pe.wait_ge(out_done, LAST.at(-1).count(2, 2))
            project_out(LAST, 0)
            project_out(LAST, 1)
            modulated(LAST, A)


_INS = ['x', 'cond_1024', 'mask_Bx1x1xS_ff0', 'L0_cond_c_attn_w', 'L0_cond_c_attn_b', 'L0_cond_c_proj_w',
        'L0_cond_c_proj_b', 'L0_cond_uk_w', 'L0_cond_uk_b', 'L0_cond_uv_w', 'L0_cond_uv_b', 'L1_cond_weight']


def kernel(**inputs):
    import numpy as _np
    import concourse.bacc as _bacc
    from concourse import mybir as _mybir
    from concourse.bass_utils import run_bass_kernel_spmd as _run

    nc = _bacc.Bacc("TRN2", target_bir_lowering=False, num_devices=1, dynamic_dma_scratch_size=1024)
    arrays, args = {}, []
    for name in _INS:
        a = _np.ascontiguousarray(inputs[name])
        arrays[f"in_{name}"] = a
        args.append(nc.dram_tensor(f"in_{name}", a.shape, _mybir.dt.from_np(a.dtype), kind="ExternalInput").ap())
    args.append(nc.dram_tensor("out_0", (NB, P, E), _mybir.dt.float32, kind="ExternalOutput").ap())
    build(nc, *args)
    r = _run(nc, [arrays], core_ids=[0])
    return r.results[0]["out_0"]
```
